# Optimizing a Trainium2 kernel written in Bass

```python
import numpy as np
import jax
import jax.numpy as jnp

def _softmax(x, axis=-1):
    return jax.nn.softmax(x, axis=axis)

def _gelu(x):
    return jax.nn.gelu(x, approximate=True)

def _silu(x):
    return jax.nn.silu(x)

def _sigmoid(x):
    return jax.nn.sigmoid(x)

def _layernorm(x, axis=-1, eps=1e-05):
    m = jnp.mean(x, axis=axis, keepdims=True)
    v = jnp.var(x, axis=axis, keepdims=True)
    return (x - m) / jnp.sqrt(v + eps)

def _scatter_add(tgt, idx, src, axis=0):
    return tgt.at[idx].add(src)

def _segment_sum(src, seg, n):
    return jax.ops.segment_sum(src, seg, n)
kernel_name = 'mk_seq_postln_d1_jaxref_r8_89a4b8'

def setup_inputs(seed: int=0):
    np.random.seed(seed)
    _w = jnp.asarray

    def _L0_attn_setup():
        import jax, jax.numpy as jnp
        import numpy as np
        NUM_HEADS = 16
        EMB = 128
        DH = 64
        B, S = (4, 256)
        key = jax.random.key(seed)
        ks = jax.random.split(key, 9)
        sc = lambda fan_in: 1.0 / np.sqrt(fan_in)
        Wq = jax.random.uniform(ks[0], (NUM_HEADS, EMB, DH), minval=-sc(EMB), maxval=sc(EMB))
        Wk = jax.random.uniform(ks[1], (NUM_HEADS, EMB, DH), minval=-sc(EMB), maxval=sc(EMB))
        Wv = jax.random.uniform(ks[2], (NUM_HEADS, EMB, DH), minval=-sc(EMB), maxval=sc(EMB))
        bq = jax.random.uniform(ks[3], (NUM_HEADS, DH), minval=-sc(EMB), maxval=sc(EMB))
        bk = jax.random.uniform(ks[4], (NUM_HEADS, DH), minval=-sc(EMB), maxval=sc(EMB))
        bv = jax.random.uniform(ks[5], (NUM_HEADS, DH), minval=-sc(EMB), maxval=sc(EMB))
        Wo = jax.random.uniform(ks[6], (NUM_HEADS * DH, EMB), minval=-sc(NUM_HEADS * DH), maxval=sc(NUM_HEADS * DH))
        bo = jax.random.uniform(ks[7], (EMB,), minval=-sc(NUM_HEADS * DH), maxval=sc(NUM_HEADS * DH))
        x = jax.random.normal(ks[8], (B, S, EMB), dtype=jnp.float32)
        return {'x': x, 'Wq': Wq, 'Wk': Wk, 'Wv': Wv, 'bq': bq, 'bk': bk, 'bv': bv, 'Wo': Wo, 'bo': bo}
    _L0_attn_in = _L0_attn_setup()

    def _L0_ffn_setup():
        import jax, jax.numpy as jnp
        import numpy as np
        E = 8
        K = 2
        D = 128
        H = 4 * D
        EPS = 1e-05
        TEMP = 1.5
        key = jax.random.key(seed)
        ks = jax.random.split(key, 6)
        B, T = (2, 256)
        x = jax.random.normal(ks[0], (B, T, D), dtype=jnp.float32)
        gamma = jnp.ones((D,), dtype=jnp.float32)
        beta = jnp.zeros((D,), dtype=jnp.float32)
        router_w = jax.random.normal(ks[1], (E, D), dtype=jnp.float32) * 0.02
        W1 = jax.random.normal(ks[2], (E, D, H), dtype=jnp.float32) * 0.02
        W2 = jax.random.normal(ks[3], (E, H, D), dtype=jnp.float32) * 0.02
        return {'x': x, 'gamma': gamma, 'beta': beta, 'router_w': router_w, 'W1': W1, 'W2': W2}
    _L0_ffn_in = _L0_ffn_setup()
    _d = {'L0_attn_x': _L0_attn_in['x'], 'L0_attn_Wq': _L0_attn_in['Wq'], 'L0_attn_Wk': _L0_attn_in['Wk'], 'L0_attn_Wv': _L0_attn_in['Wv'], 'L0_attn_bq': _L0_attn_in['bq'], 'L0_attn_bk': _L0_attn_in['bk'], 'L0_attn_bv': _L0_attn_in['bv'], 'L0_attn_Wo': _L0_attn_in['Wo'], 'L0_attn_bo': _L0_attn_in['bo'], 'L0_ffn_gamma': _L0_ffn_in['gamma'], 'L0_ffn_beta': _L0_ffn_in['beta'], 'L0_ffn_router_w': _L0_ffn_in['router_w'], 'L0_ffn_W1': _L0_ffn_in['W1'], 'L0_ffn_W2': _L0_ffn_in['W2']}
    _x0 = _d['L0_attn_x']
    _d['L0_attn_x'] = jax.random.normal(jax.random.fold_in(jax.random.key(seed), 1), (32, 256, 128), dtype=_x0.dtype)
    del _x0
    return _d

def reference(L0_attn_x, L0_attn_Wq, L0_attn_Wk, L0_attn_Wv, L0_attn_bq, L0_attn_bk, L0_attn_bv, L0_attn_Wo, L0_attn_bo, L0_ffn_gamma, L0_ffn_beta, L0_ffn_router_w, L0_ffn_W1, L0_ffn_W2):

    def _L0_attn_ref(x, Wq, Wk, Wv, bq, bk, bv, Wo, bo):
        import jax, jax.numpy as jnp
        import numpy as np
        NUM_HEADS = 16
        EMB = 128
        DH = 64
        B, S = (4, 256)
        seq_len = x.shape[1]
        q = jnp.einsum('bse,hed->bhsd', x, Wq) + bq[None, :, None, :]
        k = jnp.einsum('bse,hed->bhsd', x, Wk) + bk[None, :, None, :]
        v = jnp.einsum('bse,hed->bhsd', x, Wv) + bv[None, :, None, :]
        scores = jnp.einsum('bhsd,bhtd->bhst', q, k) / jnp.sqrt(jnp.float32(DH))
        causal = jnp.tril(jnp.ones((seq_len, seq_len), dtype=bool))
        scores = jnp.where(causal[None, None, :, :], scores, -jnp.inf)
        attn = jax.nn.softmax(scores, axis=-1)
        out = jnp.einsum('bhst,bhtd->bhsd', attn, v)
        out = out.transpose(0, 2, 1, 3).reshape(x.shape[0], seq_len, NUM_HEADS * DH)
        return out @ Wo + bo

    def _L0_ffn_ref(x, gamma, beta, router_w, W1, W2):
        import jax, jax.numpy as jnp
        import numpy as np
        E = 8
        K = 2
        D = 128
        H = 4 * D
        EPS = 1e-05
        TEMP = 1.5
        res = x
        mu = jnp.mean(x, axis=-1, keepdims=True)
        var = jnp.mean(jnp.square(x - mu), axis=-1, keepdims=True)
        xn = (x - mu) * jax.lax.rsqrt(var + EPS) * gamma + beta
        logits = jnp.einsum('btd,ed->bte', xn, router_w)
        probs = jax.nn.softmax(logits / TEMP, axis=-1)
        w, idx = jax.lax.top_k(probs, K)
        wdense = jnp.sum(jax.nn.one_hot(idx, E, dtype=w.dtype) * w[..., None], axis=-2)
        h = jax.nn.silu(jnp.einsum('btd,edf->betf', xn, W1))
        y = jnp.einsum('betf,efd->betd', h, W2)
        out = jnp.einsum('bte,betd->btd', wdense, y)
        return out + res
    x = L0_attn_x
    x = _layernorm(x + _L0_attn_ref(x, L0_attn_Wq, L0_attn_Wk, L0_attn_Wv, L0_attn_bq, L0_attn_bk, L0_attn_bv, L0_attn_Wo, L0_attn_bo), axis=-1)
    x = _layernorm(x + _L0_ffn_ref(x, L0_ffn_gamma, L0_ffn_beta, L0_ffn_router_w, L0_ffn_W1, L0_ffn_W2), axis=-1)
    return x

_drawn_inputs = setup_inputs


def setup_inputs(seed=0):
    import zlib

    import numpy as np

    out = dict(_drawn_inputs(seed))
    spreads = {'L0_ffn_gamma': (1.0, 0.6), 'L0_ffn_beta': (0.0, 0.8)}
    factors = {'L0_attn_Wq': 3.209,
     'L0_attn_Wk': 3.197,
     'L0_attn_bq': 8.0,
     'L0_attn_bk': 8.0,
     'L0_attn_bo': 2.97,
     'L0_ffn_router_w': 8.0,
     'L0_ffn_W1': 8.0,
     'L0_ffn_W2': 8.0}
    for name, (base, spread) in spreads.items():
        noise = np.random.default_rng([zlib.crc32(name.encode()), seed]).standard_normal(out[name].shape)
        drawn = base * np.exp(spread * noise) if base else spread * noise
        out[name] = jnp.asarray(drawn.astype(out[name].dtype))
    for name, factor in factors.items():
        out[name] = (out[name] * factor).astype(out[name].dtype)
    return out
```

```python
from contextlib import ExitStack

import concourse.bass as bass
from concourse import mybir

F32 = mybir.dt.float32
F32R = mybir.dt.float32r
BF16 = mybir.dt.bfloat16
U32 = mybir.dt.uint32
I32 = mybir.dt.int32
ALU = mybir.AluOpType
ACT = mybir.ActivationFunctionType
AX = mybir.AxisListType

P = 128
LAG = 4
EPS = 1e-5
ROUTER_TEMP = 1.5
MASKED = -1e30
RSQRT_SEED = 0x5F3759DF
NEWTON_STEPS = 3
PAIRS = 8


def postln_block(nc, x, wq, wk, wv, bq, bk, bv, wo, bo, gamma, beta, router_wt, w1, w2, out):
    SEQS, S, D = x.shape
    TILES = S // P
    HD = wq.shape[1]
    HEADS = 2 * PAIRS
    DH = HD // HEADS
    E = router_wt.shape[1]
    HID = w1.shape[1] // E
    CH = HID // P
    assert (S, D, DH, E, CH, TILES) == (256, P, 64, PAIRS, 4, 2)
    G = SEQS * PAIRS
    VW = 3 * DH
    SCALE = DH ** -0.5

    gate_dram = nc.dram_tensor("gate_scratch", (S, E), F32, kind="Internal").ap()

    with ExitStack() as ctx:
        def sb(name, shape, dt=F32):
            return ctx.enter_context(nc.sbuf_tensor(name, shape, dt))

        def psum(name, shape):
            return ctx.enter_context(nc.psum_tensor(name, shape, F32))

        def sem(name):
            return ctx.enter_context(nc.semaphore(name))

        w_raw = sb("w_raw", [P, E * HID])
        wqkv_raw = w_raw[:, 0:3 * HD].rearrange("p (i n) -> p i n", i=3)
        w2_raw = w_raw[:].rearrange("p (e n) -> p e n", e=E)
        wqkv_hi = sb("wqkv_hi", [P, 3, HD], F32R)
        wqkv_lo = sb("wqkv_lo", [P, 3, HD], F32R)
        wo_sb = sb("wo_sb", [P, PAIRS, D])
        w1_raw = sb("w1_raw", [P, E, HID])
        w1_hi = sb("w1_hi", [P, E, HID], F32R)
        w1_lo = sb("w1_lo", [P, E, HID], F32R)
        w2_hi = sb("w2_hi", [P, E, CH * D], F32R)
        w2_lo = sb("w2_lo", [P, E, CH * D], F32R)
        rw_sb = sb("rw_sb", [P, E])
        bq_raw = sb("bq_raw", [P, PAIRS])
        bq_sb = sb("bq_sb", [P, PAIRS])
        bk_sb = sb("bk_sb", [P, PAIRS])
        bv_sb = sb("bv_sb", [P, PAIRS])
        bo_sb = sb("bo_sb", [P, D])
        gamma_sb = sb("gamma_sb", [P, 1])
        beta_sb = sb("beta_sb", [P, 1])
        ident = sb("ident", [P, P])
        ident_bf = sb("ident_bf", [P, P], BF16)
        mask_bf = sb("mask_bf", [P, 2, P], BF16)
        expert_no = sb("expert_no", [P, E])
        x_raw = sb("x_raw", [P, TILES, D])
        xb = sb("xb", [P, TILES, D])
        xt_hi = sb("xt_hi", [P, S], F32R)
        xt_lo = sb("xt_lo", [P, S], F32R)
        qk = sb("qk", [P, 2, S])
        v_hi = sb("v_hi", [P, TILES, PAIRS, VW], F32R)
        v_lo = sb("v_lo", [P, TILES, PAIRS, VW], F32R)
        neg_max = sb("neg_max", [P, 2, 2])
        probs = sb("probs", [P, 2, 3 * P])
        sums = sb("sums", [P, 2, 2])
        inv_sums = sb("inv_sums", [P, 2, 2])
        pt_hi = sb("pt_hi", [P, 2, 3 * P], F32R)
        pt_lo = sb("pt_lo", [P, 2, 3 * P], F32R)
        ot = sb("ot", [P, PAIRS, S])
        res1 = sb("res1", [P, TILES, D])
        x1 = sb("x1", [P, TILES, D])
        x1_twice = sb("x1_twice", [P, TILES, D])
        xn = sb("xn", [P, TILES, D])
        xnt = sb("xnt", [P, S])
        xnt_hi = sb("xnt_hi", [P, S], F32R)
        xnt_lo = sb("xnt_lo", [P, S], F32R)
        ln_stats = sb("ln_stats", [P, TILES, 6])
        ln_mv = sb("ln_mv", [P, TILES, 2])
        ln_var = sb("ln_var", [P, TILES])
        ln_bits = sb("ln_bits", [P, TILES])
        ln_y = sb("ln_y", [P, TILES])
        ln_a = sb("ln_a", [P, TILES])
        ln_b = sb("ln_b", [P, TILES])
        waited = sb("waited", [P, 1])
        r_negmax = sb("r_negmax", [P, TILES])
        r_diff = sb("r_diff", [P, TILES, E])
        r_exp = sb("r_exp", [P, TILES, E])
        r_sum = sb("r_sum", [P, TILES])
        r_inv = sb("r_inv", [P, TILES])
        r_probs = sb("r_probs", [P, TILES, E])
        r_top = sb("r_top", [P, TILES, E])
        r_idx = sb("r_idx", [P, TILES, E], U32)
        r_idxf = sb("r_idxf", [P, TILES, 2])
        r_half = sb("r_half", [P, TILES, 2])
        r_first = sb("r_first", [P, TILES, E])
        r_second = sb("r_second", [P, TILES, E])
        gates = sb("gates", [P, TILES, E])
        gate_all = sb("gate_all", [P, S, E])
        hh = sb("hh", [P, 2, 2 * S])
        hh_hi = sb("hh_hi", [P, 2, 2 * S], F32R)
        hh_lo = sb("hh_lo", [P, 2, 2 * S], F32R)
        y_gated = sb("y_gated", [P, S])
        y_sum = sb("y_sum", [P, S])
        res2 = sb("res2", [P, TILES, D])
        out_sb = sb("out_sb", [P, TILES, D])

        ps_s = psum("ps_s", [P, 2, 512])
        ps_pt = psum("ps_pt", [P, 2, 512])
        ps_qk = psum("ps_qk", [P, 2, S])
        ps_z = psum("ps_z", [P, 2 * S])
        ps_y = psum("ps_y", [P, 512])
        ps_m = psum("ps_m", [P, 512])

        x_loaded = sem("x_loaded")
        attn_w_loaded = sem("attn_w_loaded")
        ffn_w_loaded = sem("ffn_w_loaded")
        small_loaded = sem("small_loaded")
        gates_stored = sem("gates_stored")
        gate_all_loaded = sem("gate_all_loaded")
        out_stored = sem("out_stored")
        out_sb_free = sem("out_sb_free")
        pool_const = sem("pool_const")
        consts_ready = sem("consts_ready")
        attn_w_hi = sem("attn_w_hi")
        attn_w_lo = sem("attn_w_lo")
        ffn_w_hi = sem("ffn_w_hi")
        ffn_w_lo = sem("ffn_w_lo")
        scores_ready = sem("scores_ready")
        pt_ready = sem("pt_ready")
        o_ready = sem("o_ready")
        qk_ready = sem("qk_ready")
        z_ready = sem("z_ready")
        y_ready = sem("y_ready")
        v_ready = sem("v_ready")
        proj_ready = sem("proj_ready")
        xnt_ready = sem("xnt_ready")
        logits_ready = sem("logits_ready")
        yt_ready = sem("yt_ready")
        xt_ready = sem("xt_ready")
        exp_done = sem("exp_done")
        pt_hi_done = sem("pt_hi_done")
        ot_done = sem("ot_done")
        qk_done = sem("qk_done")
        tanh_done = sem("tanh_done")
        v_hi_done = sem("v_hi_done")
        xt_hi_done = sem("xt_hi_done")
        xnt_done = sem("xnt_done")
        r_exp_done = sem("r_exp_done")
        max_done = sem("max_done")
        inv_done = sem("inv_done")
        probs_done = sem("probs_done")
        pt_lo_done = sem("pt_lo_done")
        hh_done = sem("hh_done")
        hh_hi_done = sem("hh_hi_done")
        y_done = sem("y_done")
        v_lo_done = sem("v_lo_done")
        xt_lo_done = sem("xt_lo_done")
        res1_done = sem("res1_done")
        x1_done = sem("x1_done")
        xn_done = sem("xn_done")
        xnt_hi_done = sem("xnt_hi_done")
        r_diff_done = sem("r_diff_done")
        gates_done = sem("gates_done")
        res2_done = sem("res2_done")
        out_done = sem("out_done")
        ln_link = sem("ln_link")
        fin_link = sem("fin_link")
        logits_link = sem("logits_link")
        r_link = sem("r_link")
        xb_done = sem("xb_done")
        hh_lo_done = sem("hh_lo_done")
        y_sum_done = sem("y_sum_done")
        xnt_lo_done = sem("xnt_lo_done")
        x1_twice_done = sem("x1_twice_done")

        block = ctx.enter_context(nc.Block())

        def iterations(eng, step):
            def one(t, n):
                for p in range(PAIRS):
                    step(t, n, p)
            one(0, 0)
            one(1, 1)
            with eng.Fori(2, SEQS - 1) as t:
                one(t, 2)
            one(SEQS - 1, SEQS - 1)
            one(SEQS, SEQS)
            one(SEQS + 1, SEQS + 1)

        def pair_in_range(n, p, off=0):
            return 0 <= PAIRS * n + p + off < G

        def pass_in_range(n, p, off=0):
            return 0 <= PAIRS * (n - 1) + p - LAG + off < G

        def g_of(t, p):
            return t * PAIRS + p

        def f_of(t, p):
            return t * PAIRS + (p - LAG - PAIRS)

        def expert(p):
            return (p - LAG) % PAIRS

        def y_sums(t, p):
            return t * (E - 1) + (expert(p - 1) - (E - 1) * (1 if p > LAG else 2))

        def v_halves(v, half, tile):
            c = PAIRS // 2
            return v[:, tile, half * c:(half + 1) * c, :].rearrange("p c (h d) -> p c h d", h=3)[:, :, 0:3:2, :]

        @block.sync
        def _(sp):
            sp.dma_start(x_raw[:], x[0].rearrange("(i p) d -> p i d", p=P)).then_inc(x_loaded, 16)
            for i, w in enumerate((wq, wk, wv)):
                sp.dma_start(wqkv_raw[:, i, :], w).then_inc(attn_w_loaded, 16)
            sp.dma_start(w1_raw[:].rearrange("p e h -> p (e h)"), w1).then_inc(ffn_w_loaded, 16)
            sp.wait_ge(attn_w_lo, 1)
            sp.dma_start(w_raw[:], w2).then_inc(ffn_w_loaded, 16)

            def step(t, n, p):
                if p == 1 and n + 1 < SEQS:
                    sp.wait_ge(xt_ready, t + 1)
                    sp.wait_ge(xb_done, t + 1)
                    sp.dma_start(x_raw[:], x[t + 1].rearrange("(i p) d -> p i d", p=P)
                                 ).then_inc(x_loaded, 16)
                if p == 4 and 1 <= n <= SEQS:
                    sp.wait_ge(gates_done, t)
                    sp.dma_start(gate_dram.rearrange("(i p) e -> p i e", p=P), gates[:]
                                 ).then_inc(gates_stored, 16)
                    sp.wait_ge(gates_stored, t * 16)
                    if n >= 2:
                        sp.wait_ge(y_done, (t - 1) * PAIRS)
                    sp.dma_start(gate_all[:].rearrange("p s e -> p (s e)"),
                                 gate_dram.rearrange("s e -> (s e)").partition_broadcast(P)
                                 ).then_inc(gate_all_loaded, 16)
                if p == 6 and n >= 2:
                    sp.wait_ge(out_done, t - 1)
                    sp.dma_start(out[t - 2].rearrange("(i p) d -> p i d", p=P), out_sb[:]
                                 ).then_inc(out_stored, 16)
                    sp.wait_ge(out_stored, (t - 1) * 16)
                    sp.sem_inc(out_sb_free, 1)

            sp.sem_inc(out_sb_free, 1)
            iterations(sp, step)
            sp.wait_ge(out_stored, 16 * SEQS)

        @block.gpsimd
        def _(pool):
            pool.memset(ident[:], 0.0).then_inc(pool_const, 1)
            pool.memset(mask_bf[:], 0.0).then_inc(pool_const, 1)
            for e in range(E):
                pool.memset(expert_no[:, e:e + 1], float(e))
            pool.memset(v_hi[:].bitcast(F32), 0.0)
            pool.memset(v_lo[:].bitcast(F32), 0.0)
            pool.wait_ge(pool_const, 2)
            pool.affine_select(out=ident[:], in_=ident[:], compare_op=ALU.not_equal, fill=1.0, base=0,
                               pattern=[[-1, P]], channel_multiplier=1).then_inc(pool_const, 1)
            pool.affine_select(out=mask_bf[:], in_=mask_bf[:], compare_op=ALU.is_ge, fill=MASKED, base=0,
                               pattern=[[0, 2], [-1, P]], channel_multiplier=1)
            pool.wait_ge(pool_const, 3)
            pool.tensor_copy(ident_bf[:], ident[:]).then_inc(consts_ready, 1)

            def split_ffn_weights(i):
                pool.wait_ge(ffn_w_hi, 2 * i + 2)
                pool.tensor_tensor(w1_lo[:, i, :], w1_raw[:, i, :], w1_hi[:, i, :].bitcast(F32),
                                   ALU.subtract)
                pool.tensor_tensor(w2_lo[:, i, :], w2_raw[:, i, :], w2_hi[:, i, :].bitcast(F32),
                                   ALU.subtract).then_inc(ffn_w_lo, 1)

            def hidden_rest(t, p, half):
                pool.wait_ge(hh_hi_done, f_of(t, p) * 2 + (half + 1))
                pool.tensor_tensor(hh_lo[:, half, :], hh[:, half, :], hh_hi[:, half, :].bitcast(F32),
                                   ALU.subtract).then_inc(hh_lo_done, 1)

            def step(t, n, p):
                if n == 0 and p >= PAIRS // 2:
                    split_ffn_weights(2 * p - PAIRS)
                    split_ffn_weights(2 * p - PAIRS + 1)
                if p == LAG and 1 <= n <= SEQS:
                    pool.wait_ge(xnt_hi_done, t)
                    pool.tensor_tensor(xnt_lo[:], xnt[:], xnt_hi[:].bitcast(F32), ALU.subtract
                                       ).then_inc(xnt_lo_done, 1)
                if pass_in_range(n, p):
                    hidden_rest(t, p, 0)
                if pass_in_range(n, p, -1) and expert(p - 1) > 0:
                    if expert(p - 1) > 1:
                        pool.wait_ge(y_sum_done, y_sums(t, p) - 1)
                    pool.wait_ge(y_done, f_of(t, p))
                    pool.tensor_tensor(y_sum[:], y_sum[:], y_gated[:], ALU.add).then_inc(y_sum_done, 1)
                if p == 1 and n < SEQS:
                    if n >= 1:
                        pool.wait_ge(res1_done, t)
                    pool.wait_ge(x_loaded, t * 16 + 16)
                    for i in range(TILES):
                        ins = pool.tensor_tensor(xb[:, i, :], x_raw[:, i, :], bo_sb[:], ALU.add)
                    ins.then_inc(xb_done, 1)
                if p == 5 and 1 <= n <= SEQS:
                    pool.wait_ge(x1_done, t)
                    if n >= 2:
                        pool.wait_ge(res2_done, t - 1)
                    pool.tensor_tensor(x1_twice[:], x1[:], x1[:], ALU.add).then_inc(x1_twice_done, 1)
                if pass_in_range(n, p):
                    hidden_rest(t, p, 1)

            pool.wait_ge(small_loaded, 16 * 8)
            iterations(pool, step)

        @block.scalar
        def _(act):
            for dst, src in ((bq_raw, bq), (bk_sb, bk), (bv_sb, bv), (bo_sb, bo), (gamma_sb, gamma),
                             (beta_sb, beta), (rw_sb, router_wt),
                             (wo_sb, wo.rearrange("p (c d) -> p c d", c=PAIRS))):
                act.dma_start(dst[:], src).then_inc(small_loaded, 16)

            def evacuate_qk(count, p):
                act.wait_ge(qk_ready, count)
                act.activation(qk[:, 0, :], ps_qk[:, 0, :], ACT.Identity, bias=bq_sb[:, p:p + 1])
                act.activation(qk[:, 1, :], ps_qk[:, 1, :], ACT.Identity, bias=bk_sb[:, p:p + 1]
                               ).then_inc(qk_done, 1)

            def v_part(t, quarter):
                half, tile = quarter // 2, quarter % 2
                act.wait_ge(v_ready, t * 4 + (quarter + 1))
                act.activation(v_halves(v_hi, half, tile), ps_m[:].rearrange("p (c h d) -> p c h d", h=2, d=DH),
                               ACT.Copy).then_inc(v_hi_done, 1)

            def split_xt(t):
                act.wait_ge(xt_ready, t + 1)
                act.activation(xt_hi[:], ps_m[:, 0:S], ACT.Copy).then_inc(xt_hi_done, 1)

            split_xt(0)
            act.wait_ge(consts_ready, 1)
            act.wait_ge(attn_w_lo, 1)
            evacuate_qk(1, 0)
            v_part(0, 0)

            def tanh_half(t, p, half):
                act.wait_ge(z_ready, f_of(t, p) * 2 + (half + 1))
                act.activation(hh[:, half, :], ps_z[:], ACT.Tanh, scale=0.5).then_inc(tanh_done, 1)

            def step(t, n, p):
                g = g_of(t, p)
                if pair_in_range(n, p, -1):
                    act.wait_ge(pt_ready, g)
                    act.activation(pt_hi[:], ps_pt[:, :, 0:3 * P], ACT.Copy).then_inc(pt_hi_done, 1)
                if p == 1 and n < SEQS:
                    v_part(t, 1)
                if p == 3 and n < SEQS:
                    v_part(t, 3)
                if pass_in_range(n, p):
                    tanh_half(t, p, 0)
                if pair_in_range(n, p):
                    act.wait_ge(max_done, g + 1)
                    for h in range(2):
                        act.activation(probs[:, h, 0:2 * P], ps_s[:, h, 0:2 * P], ACT.Exp,
                                       bias=neg_max[:, h, 0:1], accum_out=sums[:, h, 0:1])
                        ins = act.activation(probs[:, h, 2 * P:3 * P], ps_s[:, h, 2 * P:3 * P], ACT.Exp,
                                             bias=neg_max[:, h, 1:2], accum_out=sums[:, h, 1:2])
                    ins.then_inc(exp_done, 1)
                if pair_in_range(n, p, -1):
                    act.wait_ge(o_ready, g)
                    act.activation(ot[:, (p - 1) % PAIRS, :], ps_m[:, 0:S], ACT.Identity,
                                   bias=bv_sb[:, (p - 1) % PAIRS:(p - 1) % PAIRS + 1]).then_inc(ot_done, 1)
                if pass_in_range(n, p):
                    tanh_half(t, p, 1)
                if pair_in_range(n, p, 1):
                    evacuate_qk(g + 2, (p + 1) % PAIRS)
                if p == 1 and n < SEQS:
                    v_part(t, 2)
                if p == 2 and 1 <= n <= SEQS:
                    act.wait_ge(xnt_ready, t)
                    act.activation(xnt[:], ps_m[:, 0:S], ACT.Identity, scale=gamma_sb[:, 0:1],
                                   bias=beta_sb[:, 0:1]).then_inc(xnt_done, 1)
                if p == 4 and 1 <= n <= SEQS:
                    act.wait_ge(r_diff_done, t)
                    act.activation(r_exp[:], r_diff[:], ACT.Exp, scale=1.0 / ROUTER_TEMP
                                   ).then_inc(r_exp_done, 1)
                if p == 6 and n + 1 < SEQS:
                    split_xt(t + 1)
                if p == 7 and n + 1 < SEQS:
                    v_part(t + 1, 0)

            iterations(act, step)

        @block.vector
        def _(dve):
            dve.memset(waited[:], 0.0)
            for i in range(3):
                dve.wait_ge(attn_w_loaded, 16 * 3)
                if i == 0:
                    dve.tensor_scalar(wqkv_hi[:, 0, :], wqkv_raw[:, 0, :], SCALE, None, ALU.mult
                                      ).then_inc(attn_w_hi, 1)
                    dve.wait_ge(attn_w_hi, 1)
                    dve.scalar_tensor_tensor(out=wqkv_lo[:, 0, :], in0=wqkv_raw[:, 0, :], scalar=SCALE,
                                             in1=wqkv_hi[:, 0, :].bitcast(F32), op0=ALU.mult,
                                             op1=ALU.subtract)
                else:
                    dve.tensor_copy(wqkv_hi[:, i, :], wqkv_raw[:, i, :]).then_inc(attn_w_hi, 1)
                    dve.wait_ge(attn_w_hi, i + 1)
                    dve.tensor_tensor(wqkv_lo[:, i, :], wqkv_raw[:, i, :], wqkv_hi[:, i, :].bitcast(F32),
                                      ALU.subtract)
            dve.wait_ge(small_loaded, 16 * 8)
            dve.tensor_scalar(bq_sb[:], bq_raw[:], SCALE, None, ALU.mult).then_inc(attn_w_lo, 1)

            def split_xt(t):
                dve.wait_ge(xt_hi_done, t + 1)
                dve.tensor_tensor(xt_lo[:], ps_m[:, 0:S], xt_hi[:].bitcast(F32), ALU.subtract
                                  ).then_inc(xt_lo_done, 1)

            def v_part(t, quarter):
                half, tile = quarter // 2, quarter % 2
                dve.wait_ge(v_hi_done, t * 4 + (quarter + 1))
                dve.tensor_tensor(v_halves(v_lo, half, tile),
                                  ps_m[:].rearrange("p (c h d) -> p c h d", h=2, d=DH),
                                  v_halves(v_hi, half, tile).bitcast(F32), ALU.subtract
                                  ).then_inc(v_lo_done, 1)

            split_xt(0)
            v_part(0, 0)

            class Links:

                def __init__(self, s, base):
                    self.s, self.base, self.k = s, base, 0

                def __call__(self, ins):
                    ins.then_inc(self.s, 1)
                    self.k += 1
                    dve.wait_ge(self.s, self.base + self.k)

            def flat(tile):
                return tile[:].rearrange("p i d -> p (i d)")

            def hold():
                dve.memset(waited[:], 0.0)

            LINKS_PER_LN = 5 + 3 * NEWTON_STEPS

            def layer_norm(link, src, dst, done):
                for i in range(TILES):
                    ins = dve.bn_stats(ln_stats[:, i, :], src[:, i, :])
                link(ins)
                hold()
                for i in range(TILES):
                    ins = dve.bn_aggr(ln_mv[:, i, :], ln_stats[:, i, :])
                link(ins)
                link(dve.tensor_scalar(ln_var[:], ln_mv[:, :, 1], EPS, None, ALU.add))
                link(dve.tensor_scalar(ln_bits[:].bitcast(I32), ln_var[:].bitcast(I32), 1, None,
                                       ALU.logical_shift_right))
                link(dve.tensor_scalar(ln_y[:].bitcast(I32), ln_bits[:].bitcast(I32), -1, RSQRT_SEED,
                                       ALU.mult, ALU.add))
                for _ in range(NEWTON_STEPS):
                    link(dve.tensor_tensor(ln_a[:], ln_y[:], ln_y[:], ALU.mult))
                    link(dve.scalar_tensor_tensor(out=ln_b[:], in0=ln_a[:], scalar=-0.5, in1=ln_var[:],
                                                  op0=ALU.mult, op1=ALU.mult))
                    link(dve.scalar_tensor_tensor(out=ln_y[:], in0=ln_b[:], scalar=1.5, in1=ln_y[:],
                                                  op0=ALU.add, op1=ALU.mult))
                for i in range(TILES):
                    ins = dve.tensor_scalar(dst[:, i, :], src[:, i, :], ln_mv[:, i, 0:1], ln_y[:, i:i + 1],
                                            ALU.subtract, ALU.mult)
                ins.then_inc(done, 1)

            def hidden(t, p, half):
                dve.wait_ge(tanh_done, f_of(t, p) * 2 + (half + 1))
                dve.scalar_tensor_tensor(out=hh[:, half, :], in0=hh[:, half, :], scalar=1.0, in1=ps_z[:],
                                         op0=ALU.add, op1=ALU.mult).then_inc(hh_done, 1)

            def hidden_hi(t, p, half):
                dve.wait_ge(hh_done, f_of(t, p) * 2 + (half + 1))
                dve.tensor_copy(hh_hi[:, half, :], hh[:, half, :]).then_inc(hh_hi_done, 1)

            def router(t):
                link = Links(r_link, (t - 1) * ROUTER_LINKS)
                dve.wait_ge(r_exp_done, t)
                link(dve.tensor_reduce(r_sum[:], r_exp[:], AX.X, ALU.add))
                link(dve.reciprocal(r_inv[:], r_sum[:]))
                link(dve.tensor_tensor(r_probs[:], r_exp[:],
                                       r_inv[:].unsqueeze(2).to_broadcast([P, TILES, E]), ALU.mult))
                hold()
                for i in range(TILES):
                    ins = dve.max(r_top[:, i, :], r_probs[:, i, :])
                link(ins)
                hold()
                for i in range(TILES):
                    ins = dve.max_index(r_idx[:, i, :], r_top[:, i, :], r_probs[:, i, :])
                dve.tensor_scalar(r_half[:], r_top[:, :, 0:2], 0.5, None, ALU.mult)
                link(ins)
                link(dve.tensor_copy(r_idxf[:], r_idx[:, :, 0:2]))
                for i in range(TILES):
                    dve.tensor_scalar(r_first[:, i, :], expert_no[:], r_idxf[:, i, 0:1],
                                      r_half[:, i, 0:1], ALU.is_equal, ALU.mult)
                    ins = dve.tensor_scalar(r_second[:, i, :], expert_no[:], r_idxf[:, i, 1:2],
                                            r_half[:, i, 1:2], ALU.is_equal, ALU.mult)
                link(ins)
                assert link.k == ROUTER_LINKS
                dve.tensor_tensor(gates[:], r_first[:], r_second[:], ALU.add).then_inc(gates_done, 1)

            ROUTER_LINKS = 7

            def step(t, n, p):
                g, f = g_of(t, p), f_of(t, p)
                if pair_in_range(n, p, -1):
                    dve.wait_ge(pt_hi_done, g)
                    dve.tensor_tensor(pt_lo[:], ps_pt[:, :, 0:3 * P], pt_hi[:].bitcast(F32), ALU.subtract
                                      ).then_inc(pt_lo_done, 1)
                if p == 1 and n < SEQS:
                    v_part(t, 1)
                if p == 3 and n < SEQS:
                    v_part(t, 3)
                if p == 4 and 1 <= n <= SEQS:
                    dve.wait_ge(logits_ready, t)
                    logits = ps_m[:, 0:TILES * E].rearrange("p (i e) -> p i e", i=TILES)
                    dve.tensor_reduce(r_negmax[:], logits, AX.X, ALU.max, negate=True
                                      ).then_inc(logits_link, 1)
                    dve.wait_ge(logits_link, t)
                    dve.tensor_tensor(r_diff[:], logits,
                                      r_negmax[:].unsqueeze(2).to_broadcast([P, TILES, E]), ALU.add
                                      ).then_inc(r_diff_done, 1)
                if p == 5 and n >= 2:
                    dve.wait_ge(yt_ready, t - 1)
                    dve.wait_ge(x1_twice_done, t - 1)
                    dve.tensor_tensor(flat(res2), ps_m[:, 0:S], flat(x1_twice), ALU.add
                                      ).then_inc(res2_done, 1)
                if pair_in_range(n, p):
                    dve.wait_ge(scores_ready, g + 1)
                    dve.tensor_reduce(neg_max[:, :, 0], ps_s[:, :, 0:2 * P], AX.X, ALU.max, negate=True)
                    dve.tensor_reduce(neg_max[:, :, 1], ps_s[:, :, 2 * P:3 * P], AX.X, ALU.max, negate=True
                                      ).then_inc(max_done, 1)
                if pass_in_range(n, p):
                    hidden(t, p, 0)
                if pass_in_range(n, p, -1):
                    e = expert(p - 1)
                    dve.wait_ge(y_ready, f)
                    if e == 0:
                        dve.wait_ge(gate_all_loaded, t * 16)
                        if n >= 2:
                            dve.wait_ge(yt_ready, t - 1)
                    if e > 1:
                        dve.wait_ge(y_sum_done, y_sums(t, p) - 1)
                    dve.tensor_tensor(y_sum[:] if e == 0 else y_gated[:], ps_y[:, 0:S],
                                      gate_all[:, :, e], ALU.mult).then_inc(y_done, 1)
                if pass_in_range(n, p):
                    hidden_hi(t, p, 0)
                if pair_in_range(n, p):
                    dve.wait_ge(exp_done, g + 1)
                    dve.reciprocal(inv_sums[:], sums[:]).then_inc(inv_done, 1)
                    dve.wait_ge(inv_done, g + 1)
                    for h in range(2):
                        dve.tensor_scalar(probs[:, h, 0:2 * P], probs[:, h, 0:2 * P],
                                          inv_sums[:, h, 0:1], None, ALU.mult)
                        ins = dve.tensor_scalar(probs[:, h, 2 * P:3 * P], probs[:, h, 2 * P:3 * P],
                                                inv_sums[:, h, 1:2], None, ALU.mult)
                    ins.then_inc(probs_done, 1)
                if n == 0 and p >= PAIRS // 2:
                    dve.wait_ge(ffn_w_loaded, 32)
                    for e in (2 * p - PAIRS, 2 * p - PAIRS + 1):
                        dve.tensor_copy(w1_hi[:, e, :], w1_raw[:, e, :]).then_inc(ffn_w_hi, 1)
                        dve.tensor_copy(w2_hi[:, e, :], w2_raw[:, e, :]).then_inc(ffn_w_hi, 1)
                if pass_in_range(n, p):
                    hidden(t, p, 1)
                    hidden_hi(t, p, 1)
                if p == 3 and 1 <= n <= SEQS:
                    dve.wait_ge(xnt_done, t)
                    if n >= 2:
                        dve.wait_ge(z_ready, (t - 1) * (2 * PAIRS))
                    dve.tensor_copy(xnt_hi[:], xnt[:]).then_inc(xnt_hi_done, 1)
                if p == 0 and 1 <= n <= SEQS:
                    dve.wait_ge(proj_ready, t)
                    dve.wait_ge(xb_done, t)
                    dve.tensor_tensor(flat(res1), ps_m[:, 0:S], flat(xb), ALU.add).then_inc(res1_done, 1)
                if p == 1 and n < SEQS:
                    v_part(t, 2)
                if p == 1 and 1 <= n <= SEQS:
                    link = Links(ln_link, (t - 1) * (2 * LINKS_PER_LN))
                    dve.wait_ge(res1_done, t)
                    if n >= 2:
                        dve.wait_ge(x1_twice_done, t - 1)
                    layer_norm(link, res1, x1, x1_done)
                    dve.wait_ge(x1_done, t)
                    layer_norm(link, x1, xn, xn_done)
                    assert link.k == 2 * LINKS_PER_LN
                if p == 4 and 1 <= n <= SEQS:
                    router(t)
                if p == 5 and n >= 2:
                    link = Links(fin_link, (t - 2) * LINKS_PER_LN)
                    dve.wait_ge(res2_done, t - 1)
                    dve.wait_ge(out_sb_free, t - 1)
                    layer_norm(link, res2, out_sb, out_done)
                    assert link.k == LINKS_PER_LN
                if p == 6 and n + 1 < SEQS:
                    split_xt(t + 1)
                if p == 7 and n + 1 < SEQS:
                    v_part(t + 1, 0)

            iterations(dve, step)

        @block.tensor
        def _(pe):
            def product(dst, terms):
                for i, (lhs, rhs) in enumerate(terms):
                    ins = pe.matmul(dst, lhs, rhs, start=(i == 0), stop=(i == len(terms) - 1))
                return ins

            def split_terms(hi, lo, rhs_hi, rhs_lo):
                return [(hi, rhs_hi), (hi, rhs_lo), (lo, rhs_hi)]

            def transpose_tokens(src_of_tile):
                for i in range(TILES):
                    ins = pe.transpose(ps_m[:, i * P:(i + 1) * P], src_of_tile(i), ident[:])
                return ins

            def qk_projection(p):
                cols = slice(p * P, (p + 1) * P)
                for i in range(2):
                    ins = product(ps_qk[:, i, :], split_terms(wqkv_hi[:, i, cols], wqkv_lo[:, i, cols],
                                                              xt_hi[:], xt_lo[:]))
                ins.then_inc(qk_ready, 1)

            def v_projection(quarter):
                half, tile = quarter // 2, quarter % 2
                toks, cols = slice(tile * P, (tile + 1) * P), slice(half * 512, (half + 1) * 512)
                product(ps_m[:], split_terms(xt_hi[:, toks], xt_lo[:, toks], wqkv_hi[:, 2, cols],
                                             wqkv_lo[:, 2, cols])).then_inc(v_ready, 1)

            def scores():
                for h in range(2):
                    r = slice(h * DH, (h + 1) * DH)
                    pe.matmul(ps_s[:, h, 0:2 * P], qk[r, 0, P:2 * P], qk[r, 1, :], start=True, stop=True)
                for h in range(2):
                    r = slice(h * DH, (h + 1) * DH)
                    pe.matmul(ps_s[:, h, 2 * P:3 * P], qk[r, 0, 0:P], qk[r, 1, 0:P], start=False,
                              stop=True, skip_group_check=True)
                for h in range(2):
                    ins = pe.matmul(ps_s[:, h, P:3 * P], ident_bf[:], mask_bf[:].rearrange("p a b -> p (a b)"),
                                    start=False, stop=True, skip_group_check=True)
                ins.then_inc(scores_ready, 1)

            def transpose_probs():
                for h in range(2):
                    for dst, src in ((0, 2 * P), (P, 0), (2 * P, P)):
                        ins = pe.transpose(ps_pt[:, h, dst:dst + P], probs[:, h, src:src + P], ident[:])
                ins.then_inc(pt_ready, 1)

            def attention_output(p):
                n_mm = 0
                for h in range(2):
                    cols = slice(h * DH, h * DH + P)
                    key_tiles = ((0, slice(0, 2 * P), slice(0, 2 * P)), (1, slice(P, 2 * P), slice(2 * P, 3 * P)))
                    for tile, dst, src in key_tiles if h == 0 else reversed(key_tiles):
                        vh, vl = v_hi[:, tile, p, cols], v_lo[:, tile, p, cols]
                        for lhs, rhs in split_terms(vh, vl, pt_hi[:, h, src], pt_lo[:, h, src]):
                            ins = pe.matmul(ps_m[:, dst], lhs, rhs, start=(n_mm == 0), stop=(n_mm == 11))
                            n_mm += 1
                ins.then_inc(o_ready, 1)

            def hidden_projection(e, half):
                for i in range(2):
                    cols = slice((2 * half + i) * P, (2 * half + i + 1) * P)
                    ins = product(ps_z[:, i * S:(i + 1) * S],
                                  split_terms(w1_hi[:, e, cols], w1_lo[:, e, cols], xnt_hi[:], xnt_lo[:]))
                ins.then_inc(z_ready, 1)

            def expert_output(e, half):
                terms = []
                for i in range(2):
                    c = slice((2 * half + i) * D, (2 * half + i + 1) * D)
                    toks = slice(i * S, (i + 1) * S)
                    terms += split_terms(w2_hi[:, e, c], w2_lo[:, e, c], hh_hi[:, half, toks],
                                         hh_lo[:, half, toks])
                for i, (lhs, rhs) in enumerate(terms):
                    ins = pe.matmul(ps_y[:, 0:S], lhs, rhs, start=(half == 0 and i == 0),
                                    stop=(half == 1 and i == len(terms) - 1))
                if half == 1:
                    ins.then_inc(y_ready, 1)

            def wait_bank_before_attention(t, n, p):
                g = g_of(t, p)
                if p in (0, 1, 2, 3) and n < SEQS:
                    pe.wait_ge(v_lo_done, t * 4 + (p + 1))
                elif p == 4 and n >= 1:
                    pe.wait_ge(r_diff_done, t)
                elif p == 5 and n >= 2:
                    pe.wait_ge(res2_done, t - 1)
                elif p == 7 and n + 1 < SEQS:
                    pe.wait_ge(xt_lo_done, t + 2)
                else:
                    pe.wait_ge(ot_done, g - 1)

            def short_stage(t, n, p):
                g = g_of(t, p)
                mid = 1 <= n <= SEQS
                if p == 0 and mid:
                    pe.wait_ge(ot_done, g)
                    for i in range(TILES):
                        ins = product(ps_m[:, i * P:(i + 1) * P],
                                      [(ot[:, c, i * P:(i + 1) * P], wo_sb[:, c, :]) for c in range(PAIRS)])
                    ins.then_inc(proj_ready, 1)
                if p == 1 and n < SEQS:
                    pe.wait_ge(ot_done, g)
                    v_projection(2)
                if p == 2 and mid:
                    if n < SEQS:
                        pe.wait_ge(ot_done, g)
                    pe.wait_ge(xn_done, t)
                    transpose_tokens(lambda i: xn[:, i, :]).then_inc(xnt_ready, 1)
                if p == 3 and mid:
                    if n < SEQS:
                        pe.wait_ge(ot_done, g)
                    pe.wait_ge(xnt_done, t)
                    for i in range(TILES):
                        ins = pe.matmul(ps_m[:, i * E:(i + 1) * E], xnt[:, i * P:(i + 1) * P], rw_sb[:],
                                        start=True, stop=True)
                    ins.then_inc(logits_ready, 1)
                if p == 4 and n >= 2:
                    if n < SEQS:
                        pe.wait_ge(ot_done, g)
                    elif n == SEQS:
                        pe.wait_ge(r_diff_done, t)
                    pe.wait_ge(y_sum_done, (t - 1) * (E - 1))
                    transpose_tokens(lambda i: y_sum[:, i * P:(i + 1) * P]).then_inc(yt_ready, 1)
                if p == 6 and n + 1 < SEQS:
                    pe.wait_ge(ot_done, g)
                    pe.wait_ge(x_loaded, t * 16 + 32)
                    transpose_tokens(lambda i: x_raw[:, i, :]).then_inc(xt_ready, 1)
                if p == 7 and n + 1 < SEQS:
                    pe.wait_ge(ot_done, g)
                    v_projection(0)

            def late_stage(t, n, p):
                if p == 0 and n < SEQS:
                    if n >= 1:
                        pe.wait_ge(res1_done, t)
                    else:
                        pe.wait_ge(v_lo_done, 1)
                    v_projection(1)
                if p == 2 and n < SEQS:
                    if n >= 1:
                        pe.wait_ge(xnt_done, t)
                    else:
                        pe.wait_ge(ot_done, g_of(t, p))
                    v_projection(3)

            def step(t, n, p):
                g, f, e = g_of(t, p), f_of(t, p), expert(p)
                if pair_in_range(n, p):
                    pe.wait_ge(qk_done, g + 1)
                    if not (n == 0 and p == 0):
                        pe.wait_ge(exp_done, g)
                    scores()
                if pass_in_range(n, p):
                    if p == LAG:
                        pe.wait_ge(xnt_lo_done, t)
                        if n == 1:
                            pe.wait_ge(ffn_w_lo, E)
                    if not (n == 1 and p == LAG):
                        pe.wait_ge(hh_done, f * 2)
                    hidden_projection(e, 0)
                if pass_in_range(n, p, -1):
                    pe.wait_ge(hh_lo_done, f * 2)
                    expert_output(expert(p - 1), 1)
                if pair_in_range(n, p, -1):
                    pe.wait_ge(pt_lo_done, g)
                    wait_bank_before_attention(t, n, p)
                    attention_output((p - 1) % PAIRS)
                if pass_in_range(n, p):
                    pe.wait_ge(hh_done, f * 2 + 1)
                    hidden_projection(e, 1)
                if pair_in_range(n, p, 1):
                    pe.wait_ge(qk_done, g + 1)
                    if p == 7:
                        pe.wait_ge(xt_lo_done, t + 2)
                    qk_projection((p + 1) % PAIRS)
                if pass_in_range(n, p):
                    if not (n == 1 and p == LAG):
                        pe.wait_ge(y_done, f)
                    pe.wait_ge(hh_lo_done, f * 2 + 1)
                    expert_output(e, 0)
                short_stage(t, n, p)
                if pair_in_range(n, p):
                    pe.wait_ge(probs_done, g + 1)
                    transpose_probs()
                late_stage(t, n, p)

            pe.wait_ge(consts_ready, 1)
            pe.wait_ge(x_loaded, 16)
            transpose_tokens(lambda i: x_raw[:, i, :]).then_inc(xt_ready, 1)
            pe.wait_ge(attn_w_lo, 1)
            pe.wait_ge(xt_lo_done, 1)
            qk_projection(0)
            v_projection(0)
            iterations(pe, step)


def kernel(L0_attn_x, L0_attn_Wq, L0_attn_Wk, L0_attn_Wv, L0_attn_bq, L0_attn_bk, L0_attn_bv, L0_attn_Wo,
           L0_attn_bo, L0_ffn_gamma, L0_ffn_beta, L0_ffn_router_w, L0_ffn_W1, L0_ffn_W2):
    import numpy as np
    import concourse.bacc as bacc
    from concourse.bass_utils import run_bass_kernel_spmd

    def columns(a, n):
        a = np.asarray(a)
        return a.reshape(n, P, -1).transpose(1, 0, 2).reshape(P, -1)

    def by_input(w):
        w = np.asarray(w)
        return w.transpose(1, 0, 2).reshape(P, -1)

    ins = {
        "x": L0_attn_x,
        "wq": by_input(L0_attn_Wq), "wk": by_input(L0_attn_Wk), "wv": by_input(L0_attn_Wv),
        "bq": columns(L0_attn_bq, PAIRS), "bk": columns(L0_attn_bk, PAIRS), "bv": columns(L0_attn_bv, PAIRS),
        "wo": columns(L0_attn_Wo, PAIRS),
        "bo": np.broadcast_to(np.asarray(L0_attn_bo), (P, P)),
        "gamma": np.asarray(L0_ffn_gamma).reshape(P, 1), "beta": np.asarray(L0_ffn_beta).reshape(P, 1),
        "router_wt": np.asarray(L0_ffn_router_w).T,
        "w1": by_input(L0_ffn_W1),
        "w2": columns(L0_ffn_W2, np.asarray(L0_ffn_W2).size // (P * P)),
    }
    nc = bacc.Bacc("TRN2", target_bir_lowering=False, num_devices=1)
    arrays, args = {}, []
    for name, a in ins.items():
        a = np.ascontiguousarray(a)
        arrays["in_" + name] = a
        args.append(nc.dram_tensor("in_" + name, a.shape, mybir.dt.from_np(a.dtype), kind="ExternalInput").ap())
    shape = arrays["in_x"].shape
    out = nc.dram_tensor("out_x", shape, F32, kind="ExternalOutput").ap()
    postln_block(nc, *args, out)
    r = run_bass_kernel_spmd(nc, [arrays], core_ids=[0])
    return r.results[0]["out_x"]
```

```python
from contextlib import ExitStack

import concourse.bass as bass
from concourse import mybir

F32 = mybir.dt.float32
F32R = mybir.dt.float32r
BF16 = mybir.dt.bfloat16
U32 = mybir.dt.uint32
I32 = mybir.dt.int32
ALU = mybir.AluOpType
ACT = mybir.ActivationFunctionType
AX = mybir.AxisListType

P = 128
LAG = 6
EPS = 1e-5
ROUTER_TEMP = 1.5
MASKED = -1e30
RSQRT_SEED = 0x5F3759DF
NEWTON_STEPS = 3
PAIRS = 8


def postln_block(nc, x, wq, wk, wv, bq, bk, bv, wo, bo, gamma, beta, router_wt, w1, w2, out):
    SEQS, S, D = x.shape
    TILES = S // P
    HD = wq.shape[1]
    HEADS = 2 * PAIRS
    DH = HD // HEADS
    E = router_wt.shape[1]
    HID = w1.shape[1] // E
    CH = HID // P
    assert (S, D, DH, E, CH, TILES) == (256, P, 64, PAIRS, 4, 2)
    G = SEQS * PAIRS
    SCALE = DH ** -0.5

    gate_dram = nc.dram_tensor("gate_scratch", (S, E), F32, kind="Internal").ap()

    with ExitStack() as ctx:
        def sb(name, shape, dt=F32):
            return ctx.enter_context(nc.sbuf_tensor(name, shape, dt))

        def psum(name, shape):
            return ctx.enter_context(nc.psum_tensor(name, shape, F32))

        def sem(name):
            return ctx.enter_context(nc.semaphore(name))

        w_raw = sb("w_raw", [P, E * HID])
        wqkv_raw = w_raw[:, 0:3 * HD].rearrange("p (i n) -> p i n", i=3)
        w2_raw = w_raw[:].rearrange("p (e n) -> p e n", e=E)
        wqkv_hi = sb("wqkv_hi", [P, 3, HD], F32R)
        wqkv_lo = sb("wqkv_lo", [P, 3, HD], F32R)
        wo_sb = sb("wo_sb", [P, PAIRS, D])
        w1_raw = sb("w1_raw", [P, E, HID])
        w1_hi = sb("w1_hi", [P, E, HID], F32R)
        w1_lo = sb("w1_lo", [P, E, HID], F32R)
        w2_hi = sb("w2_hi", [P, E, CH * D], F32R)
        w2_lo = sb("w2_lo", [P, E, CH * D], F32R)
        rw_sb = sb("rw_sb", [P, E])
        bq_raw = sb("bq_raw", [P, PAIRS])
        bq_sb = sb("bq_sb", [P, PAIRS])
        bk_sb = sb("bk_sb", [P, PAIRS])
        bv_sb = sb("bv_sb", [P, PAIRS])
        bo_sb = sb("bo_sb", [P, D])
        gamma_sb = sb("gamma_sb", [P, 1])
        beta_sb = sb("beta_sb", [P, 1])
        ident = sb("ident", [P, P])
        ident_bf = sb("ident_bf", [P, P], BF16)
        mask_bf = sb("mask_bf", [P, 2, P], BF16)
        expert_no = sb("expert_no", [P, E])
        x_raw = sb("x_raw", [P, TILES, D])
        xb = sb("xb", [P, TILES, D])
        xt_hi = sb("xt_hi", [P, S], F32R)
        xt_lo = sb("xt_lo", [P, S], F32R)
        qk = sb("qk", [P, 2, S])
        v_hi = sb("v_hi", [P, TILES, HD], F32R)
        v_lo = sb("v_lo", [P, TILES, HD], F32R)
        neg_max = sb("neg_max", [P, 2, 2])
        probs = sb("probs", [P, 2, 3 * P])
        sums = sb("sums", [P, 2, 2])
        inv_sums = sb("inv_sums", [P, 2, 2])
        pt_hi = sb("pt_hi", [P, 2, 3 * P], F32R)
        pt_lo = sb("pt_lo", [P, 2, 3 * P], F32R)
        ot = sb("ot", [P, PAIRS, S])
        res1 = sb("res1", [P, TILES, D])
        x1 = sb("x1", [P, TILES, D])
        x1_twice = sb("x1_twice", [P, TILES, D])
        xn = sb("xn", [P, TILES, D])
        xnt = sb("xnt", [P, S])
        xnt_hi = sb("xnt_hi", [P, S], F32R)
        xnt_lo = sb("xnt_lo", [P, S], F32R)
        ln_stats = sb("ln_stats", [P, TILES, 6])
        ln_mv = sb("ln_mv", [P, TILES, 2])
        ln_var = sb("ln_var", [P, TILES])
        ln_bits = sb("ln_bits", [P, TILES])
        ln_y = sb("ln_y", [P, TILES])
        ln_a = sb("ln_a", [P, TILES])
        ln_half = sb("ln_half", [P, TILES])
        waited = sb("waited", [P, 1])
        r_negmax = sb("r_negmax", [P, TILES])
        r_diff = sb("r_diff", [P, TILES, E])
        r_exp = sb("r_exp", [P, TILES, E])
        r_sum = sb("r_sum", [P, TILES])
        r_inv = sb("r_inv", [P, TILES])
        r_probs = sb("r_probs", [P, TILES, E])
        r_top = sb("r_top", [P, TILES, E])
        r_idx = sb("r_idx", [P, TILES, E], U32)
        r_idxf = sb("r_idxf", [P, TILES, 2])
        r_half = sb("r_half", [P, TILES, 2])
        r_first = sb("r_first", [P, TILES, E])
        r_second = sb("r_second", [P, TILES, E])
        gates = sb("gates", [P, TILES, E])
        gate_all = sb("gate_all", [P, S, E])
        hh = sb("hh", [P, 2, 2 * S])
        hh_hi = sb("hh_hi", [P, 2, 2 * S], F32R)
        hh_lo = sb("hh_lo", [P, 2, 2 * S], F32R)
        y_gated = sb("y_gated", [P, S])
        y_sum = sb("y_sum", [P, S])
        res2 = sb("res2", [P, TILES, D])
        out_sb = sb("out_sb", [P, TILES, D])

        ps_s = psum("ps_s", [P, 2, 512])
        ps_pt = psum("ps_pt", [P, 2, 512])
        ps_qk = psum("ps_qk", [P, 2, S])
        ps_z = psum("ps_z", [P, 2 * S])
        ps_y = psum("ps_y", [P, 512])
        ps_m = psum("ps_m", [P, 512])

        x_loaded = sem("x_loaded")
        attn_w_loaded = sem("attn_w_loaded")
        ffn_w_loaded = sem("ffn_w_loaded")
        small_loaded = sem("small_loaded")
        gates_stored = sem("gates_stored")
        gate_all_loaded = sem("gate_all_loaded")
        out_stored = sem("out_stored")
        out_sb_free = sem("out_sb_free")
        pool_const = sem("pool_const")
        consts_ready = sem("consts_ready")
        attn_w_hi = sem("attn_w_hi")
        attn_w_lo = sem("attn_w_lo")
        ffn_w_hi = sem("ffn_w_hi")
        ffn_w_lo = sem("ffn_w_lo")
        scores_ready = sem("scores_ready")
        pt_ready = sem("pt_ready")
        o_ready = sem("o_ready")
        qk_ready = sem("qk_ready")
        z_ready = sem("z_ready")
        y_ready = sem("y_ready")
        v_ready = sem("v_ready")
        proj_ready = sem("proj_ready")
        xnt_ready = sem("xnt_ready")
        logits_ready = sem("logits_ready")
        yt_ready = sem("yt_ready")
        xt_ready = sem("xt_ready")
        exp_done = sem("exp_done")
        pt_hi_done = sem("pt_hi_done")
        ot_done = sem("ot_done")
        qk_done = sem("qk_done")
        tanh_done = sem("tanh_done")
        v_hi_done = sem("v_hi_done")
        xt_hi_done = sem("xt_hi_done")
        xnt_done = sem("xnt_done")
        r_exp_done = sem("r_exp_done")
        max_done = sem("max_done")
        inv_done = sem("inv_done")
        probs_done = sem("probs_done")
        pt_lo_done = sem("pt_lo_done")
        hh_done = sem("hh_done")
        hh_hi_done = sem("hh_hi_done")
        y_done = sem("y_done")
        v_lo_done = sem("v_lo_done")
        xt_lo_done = sem("xt_lo_done")
        res1_done = sem("res1_done")
        x1_done = sem("x1_done")
        xn_done = sem("xn_done")
        xnt_hi_done = sem("xnt_hi_done")
        r_diff_done = sem("r_diff_done")
        gates_done = sem("gates_done")
        res2_done = sem("res2_done")
        out_done = sem("out_done")
        ln_link = sem("ln_link")
        fin_link = sem("fin_link")
        logits_link = sem("logits_link")
        r_link = sem("r_link")
        xb_done = sem("xb_done")
        hh_lo_done = sem("hh_lo_done")
        y_sum_done = sem("y_sum_done")
        xnt_lo_done = sem("xnt_lo_done")
        x1_twice_done = sem("x1_twice_done")

        block = ctx.enter_context(nc.Block())

        def iterations(eng, step):
            def one(t, n):
                for p in range(PAIRS):
                    step(t, n, p)
            one(0, 0)
            one(1, 1)
            with eng.Fori(2, SEQS - 1) as t:
                one(t, 2)
            one(SEQS - 1, SEQS - 1)
            one(SEQS, SEQS)
            one(SEQS + 1, SEQS + 1)

        def pair_in_range(n, p, off=0):
            return 0 <= PAIRS * n + p + off < G

        def pass_in_range(n, p, off=0):
            return 0 <= PAIRS * (n - 1) + p - LAG + off < G

        def g_of(t, p):
            return t * PAIRS + p

        def f_of(t, p):
            return t * PAIRS + (p - LAG - PAIRS)

        def expert(p):
            return (p - LAG) % PAIRS

        def y_sums(t, p):
            return t * (E - 1) + (expert(p - 1) - (E - 1) * (1 if p > LAG else 2))

        @block.sync
        def _(sp):
            sp.dma_start(x_raw[:], x[0].rearrange("(i p) d -> p i d", p=P)).then_inc(x_loaded, 16)
            for i, w in enumerate((wq, wk, wv)):
                sp.dma_start(wqkv_raw[:, i, :], w).then_inc(attn_w_loaded, 16)
            sp.dma_start(w1_raw[:].rearrange("p e h -> p (e h)"), w1).then_inc(ffn_w_loaded, 16)
            sp.wait_ge(attn_w_lo, 1)
            sp.dma_start(w_raw[:], w2).then_inc(ffn_w_loaded, 16)

            def step(t, n, p):
                if p == 1 and n + 1 < SEQS:
                    sp.wait_ge(xt_ready, t + 1)
                    sp.wait_ge(xb_done, t + 1)
                    sp.dma_start(x_raw[:], x[t + 1].rearrange("(i p) d -> p i d", p=P)
                                 ).then_inc(x_loaded, 16)
                if p == 6 and 1 <= n <= SEQS:
                    sp.wait_ge(gates_done, t)
                    sp.dma_start(gate_dram.rearrange("(i p) e -> p i e", p=P), gates[:]
                                 ).then_inc(gates_stored, 16)
                    sp.wait_ge(gates_stored, t * 16)
                    if n >= 2:
                        sp.wait_ge(y_done, (t - 1) * PAIRS)
                    sp.dma_start(gate_all[:].rearrange("p s e -> p (s e)"),
                                 gate_dram.rearrange("s e -> (s e)").partition_broadcast(P)
                                 ).then_inc(gate_all_loaded, 16)
                if p == 7 and n >= 2:
                    sp.wait_ge(out_done, t - 1)
                    sp.dma_start(out[t - 2].rearrange("(i p) d -> p i d", p=P), out_sb[:]
                                 ).then_inc(out_stored, 16)
                    sp.wait_ge(out_stored, (t - 1) * 16)
                    sp.sem_inc(out_sb_free, 1)

            sp.sem_inc(out_sb_free, 1)
            iterations(sp, step)
            sp.wait_ge(out_stored, 16 * SEQS)

        @block.gpsimd
        def _(pool):
            pool.memset(ident[:], 0.0).then_inc(pool_const, 1)
            pool.memset(mask_bf[:], 0.0).then_inc(pool_const, 1)
            for e in range(E):
                pool.memset(expert_no[:, e:e + 1], float(e))
            pool.wait_ge(pool_const, 2)
            pool.affine_select(out=ident[:], in_=ident[:], compare_op=ALU.not_equal, fill=1.0, base=0,
                               pattern=[[-1, P]], channel_multiplier=1).then_inc(pool_const, 1)
            pool.affine_select(out=mask_bf[:], in_=mask_bf[:], compare_op=ALU.is_ge, fill=MASKED, base=0,
                               pattern=[[0, 2], [-1, P]], channel_multiplier=1)
            pool.wait_ge(pool_const, 3)
            pool.tensor_copy(ident_bf[:], ident[:]).then_inc(consts_ready, 1)

            def split_ffn_weights(i):
                pool.wait_ge(ffn_w_hi, 2 * i + 2)
                pool.tensor_tensor(w1_lo[:, i, :], w1_raw[:, i, :], w1_hi[:, i, :].bitcast(F32),
                                   ALU.subtract)
                pool.tensor_tensor(w2_lo[:, i, :], w2_raw[:, i, :], w2_hi[:, i, :].bitcast(F32),
                                   ALU.subtract).then_inc(ffn_w_lo, 1)

            def hidden_rest(t, p, half):
                pool.wait_ge(hh_hi_done, f_of(t, p) * 2 + (half + 1))
                pool.tensor_tensor(hh_lo[:, half, :], hh[:, half, :], hh_hi[:, half, :].bitcast(F32),
                                   ALU.subtract).then_inc(hh_lo_done, 1)

            def step(t, n, p):
                if n == 0 and p >= PAIRS // 2:
                    split_ffn_weights(2 * p - PAIRS)
                    split_ffn_weights(2 * p - PAIRS + 1)
                if p == LAG and 1 <= n <= SEQS:
                    pool.wait_ge(xnt_hi_done, t)
                    pool.tensor_tensor(xnt_lo[:], xnt[:], xnt_hi[:].bitcast(F32), ALU.subtract
                                       ).then_inc(xnt_lo_done, 1)
                if pass_in_range(n, p):
                    hidden_rest(t, p, 0)
                if pass_in_range(n, p, -1) and expert(p - 1) > 0:
                    if expert(p - 1) > 1:
                        pool.wait_ge(y_sum_done, y_sums(t, p) - 1)
                    pool.wait_ge(y_done, f_of(t, p))
                    pool.tensor_tensor(y_sum[:], y_sum[:], y_gated[:], ALU.add).then_inc(y_sum_done, 1)
                if p == 1 and n < SEQS:
                    if n >= 1:
                        pool.wait_ge(res1_done, t)
                    pool.wait_ge(x_loaded, t * 16 + 16)
                    for i in range(TILES):
                        ins = pool.tensor_tensor(xb[:, i, :], x_raw[:, i, :], bo_sb[:], ALU.add)
                    ins.then_inc(xb_done, 1)
                if p == 7 and 1 <= n <= SEQS:
                    pool.wait_ge(x1_done, t)
                    if n >= 2:
                        pool.wait_ge(res2_done, t - 1)
                    pool.tensor_tensor(x1_twice[:], x1[:], x1[:], ALU.add).then_inc(x1_twice_done, 1)
                if pass_in_range(n, p):
                    hidden_rest(t, p, 1)

            pool.wait_ge(small_loaded, 16 * 8)
            iterations(pool, step)

        @block.scalar
        def _(act):
            for dst, src in ((bq_raw, bq), (bk_sb, bk), (bv_sb, bv), (bo_sb, bo), (gamma_sb, gamma),
                             (beta_sb, beta), (rw_sb, router_wt),
                             (wo_sb, wo.rearrange("p (c d) -> p c d", c=PAIRS))):
                act.dma_start(dst[:], src).then_inc(small_loaded, 16)

            def evacuate_qk(count, p):
                act.wait_ge(qk_ready, count)
                act.activation(qk[:, 0, :], ps_qk[:, 0, :], ACT.Identity, bias=bq_sb[:, p:p + 1])
                act.activation(qk[:, 1, :], ps_qk[:, 1, :], ACT.Identity, bias=bk_sb[:, p:p + 1]
                               ).then_inc(qk_done, 1)

            def v_part(t, quarter):
                half, tile = quarter // 2, quarter % 2
                act.wait_ge(v_ready, t * 4 + (quarter + 1))
                act.activation(v_hi[:, tile, half * 512:(half + 1) * 512], ps_m[:], ACT.Copy
                               ).then_inc(v_hi_done, 1)

            def split_xt(t):
                act.wait_ge(xt_ready, t + 1)
                act.activation(xt_hi[:], ps_m[:, 0:S], ACT.Copy).then_inc(xt_hi_done, 1)

            split_xt(0)
            act.wait_ge(attn_w_lo, 1)
            evacuate_qk(1, 0)
            v_part(0, 0)

            def tanh_half(t, p, half):
                act.wait_ge(z_ready, f_of(t, p) * 2 + (half + 1))
                act.activation(hh[:, half, :], ps_z[:], ACT.Tanh, scale=0.5).then_inc(tanh_done, 1)

            def step(t, n, p):
                g = g_of(t, p)
                if pair_in_range(n, p, -1):
                    act.wait_ge(pt_ready, g)
                    act.activation(pt_hi[:], ps_pt[:, :, 0:3 * P], ACT.Copy).then_inc(pt_hi_done, 1)
                if p == 1 and n < SEQS:
                    v_part(t, 1)
                if p == 5 and 1 <= n <= SEQS:
                    act.wait_ge(r_diff_done, t)
                    act.activation(r_exp[:], r_diff[:], ACT.Exp, scale=1.0 / ROUTER_TEMP
                                   ).then_inc(r_exp_done, 1)
                if p == 7 and n + 1 < SEQS:
                    split_xt(t + 1)
                if pass_in_range(n, p):
                    tanh_half(t, p, 0)
                if pair_in_range(n, p):
                    act.wait_ge(max_done, g + 1)
                    for h in range(2):
                        act.activation(probs[:, h, 0:2 * P], ps_s[:, h, 0:2 * P], ACT.Exp,
                                       bias=neg_max[:, h, 0:1], accum_out=sums[:, h, 0:1])
                        ins = act.activation(probs[:, h, 2 * P:3 * P], ps_s[:, h, 2 * P:3 * P], ACT.Exp,
                                             bias=neg_max[:, h, 1:2], accum_out=sums[:, h, 1:2])
                    ins.then_inc(exp_done, 1)
                if pair_in_range(n, p, -1):
                    act.wait_ge(o_ready, g)
                    q = (p - 1) % PAIRS
                    for h in range(2):
                        r = slice(h * DH, (h + 1) * DH)
                        ins = act.activation(ot[r, q, :], ps_m[r, h * S:(h + 1) * S], ACT.Identity,
                                             bias=bv_sb[r, q:q + 1])
                    ins.then_inc(ot_done, 1)
                if pass_in_range(n, p):
                    tanh_half(t, p, 1)
                if pair_in_range(n, p, 1):
                    evacuate_qk(g + 2, (p + 1) % PAIRS)
                if p in (1, 2) and n < SEQS:
                    v_part(t, p + 1)
                if p == 3 and 1 <= n <= SEQS:
                    act.wait_ge(xnt_ready, t)
                    act.activation(xnt[:], ps_m[:, 0:S], ACT.Identity, scale=gamma_sb[:, 0:1],
                                   bias=beta_sb[:, 0:1]).then_inc(xnt_done, 1)
                if p == 7 and n + 1 < SEQS:
                    v_part(t + 1, 0)

            iterations(act, step)

        @block.vector
        def _(dve):
            dve.memset(waited[:], 0.0)
            for i in range(3):
                dve.wait_ge(attn_w_loaded, 16 * 3)
                if i == 0:
                    dve.tensor_scalar(wqkv_hi[:, 0, :], wqkv_raw[:, 0, :], SCALE, None, ALU.mult
                                      ).then_inc(attn_w_hi, 1)
                    dve.wait_ge(attn_w_hi, 1)
                    dve.scalar_tensor_tensor(out=wqkv_lo[:, 0, :], in0=wqkv_raw[:, 0, :], scalar=SCALE,
                                             in1=wqkv_hi[:, 0, :].bitcast(F32), op0=ALU.mult,
                                             op1=ALU.subtract)
                else:
                    dve.tensor_copy(wqkv_hi[:, i, :], wqkv_raw[:, i, :]).then_inc(attn_w_hi, 1)
                    dve.wait_ge(attn_w_hi, i + 1)
                    dve.tensor_tensor(wqkv_lo[:, i, :], wqkv_raw[:, i, :], wqkv_hi[:, i, :].bitcast(F32),
                                      ALU.subtract)
            dve.wait_ge(small_loaded, 16 * 8)
            dve.tensor_scalar(bq_sb[:], bq_raw[:], SCALE, None, ALU.mult).then_inc(attn_w_lo, 1)

            def split_xt(t):
                dve.wait_ge(xt_hi_done, t + 1)
                dve.tensor_tensor(xt_lo[:], ps_m[:, 0:S], xt_hi[:].bitcast(F32), ALU.subtract
                                  ).then_inc(xt_lo_done, 1)

            def v_part(t, quarter):
                half, tile = quarter // 2, quarter % 2
                dve.wait_ge(v_hi_done, t * 4 + (quarter + 1))
                cols = slice(half * 512, (half + 1) * 512)
                dve.tensor_tensor(v_lo[:, tile, cols], ps_m[:], v_hi[:, tile, cols].bitcast(F32),
                                  ALU.subtract).then_inc(v_lo_done, 1)

            split_xt(0)
            v_part(0, 0)

            def flat(tile):
                return tile[:].rearrange("p i d -> p (i d)")

            def hold():
                dve.memset(waited[:], 0.0)

            NORM_PARTS = 5 + 2 * NEWTON_STEPS

            def norm_part(k, link, count, src):
                if k > 0:
                    dve.wait_ge(link, count + k)
                if k == 0:
                    for i in range(TILES):
                        ins = dve.bn_stats(ln_stats[:, i, :], src[:, i, :])
                elif k == 1:
                    hold()
                    for i in range(TILES):
                        ins = dve.bn_aggr(ln_mv[:, i, :], ln_stats[:, i, :])
                elif k == 2:
                    ins = dve.tensor_scalar(ln_var[:], ln_mv[:, :, 1], EPS, None, ALU.add)
                elif k == 3:
                    dve.tensor_scalar(ln_half[:], ln_var[:], -0.5, None, ALU.mult)
                    ins = dve.tensor_scalar(ln_bits[:].bitcast(I32), ln_var[:].bitcast(I32), 1, None,
                                            ALU.logical_shift_right)
                elif k == 4:
                    ins = dve.tensor_scalar(ln_y[:].bitcast(I32), ln_bits[:].bitcast(I32), -1, RSQRT_SEED,
                                            ALU.mult, ALU.add)
                elif k % 2 == 1:
                    for i in range(TILES):
                        ins = dve.scalar_tensor_tensor(out=ln_a[:, i:i + 1], in0=ln_y[:, i:i + 1],
                                                       scalar=ln_half[:, i:i + 1], in1=ln_y[:, i:i + 1],
                                                       op0=ALU.mult, op1=ALU.mult)
                else:
                    ins = dve.scalar_tensor_tensor(out=ln_y[:], in0=ln_a[:], scalar=1.5, in1=ln_y[:],
                                                   op0=ALU.add, op1=ALU.mult)
                ins.then_inc(link, 1)

            def norm_end(link, count, src, dst, done):
                dve.wait_ge(link, count + NORM_PARTS)
                for i in range(TILES):
                    ins = dve.tensor_scalar(dst[:, i, :], src[:, i, :], ln_mv[:, i, 0:1], ln_y[:, i:i + 1],
                                            ALU.subtract, ALU.mult)
                ins.then_inc(done, 1)

            def hidden(t, p, half):
                dve.wait_ge(tanh_done, f_of(t, p) * 2 + (half + 1))
                dve.scalar_tensor_tensor(out=hh[:, half, :], in0=hh[:, half, :], scalar=1.0, in1=ps_z[:],
                                         op0=ALU.add, op1=ALU.mult).then_inc(hh_done, 1)

            def hidden_hi(t, p, half):
                dve.wait_ge(hh_done, f_of(t, p) * 2 + (half + 1))
                dve.tensor_copy(hh_hi[:, half, :], hh[:, half, :]).then_inc(hh_hi_done, 1)

            ROUTER_PARTS = 8

            def router_part(k, t):
                if k == 0:
                    dve.wait_ge(r_exp_done, t)
                    ins = dve.tensor_reduce(r_sum[:], r_exp[:], AX.X, ALU.add)
                else:
                    dve.wait_ge(r_link, (t - 1) * (ROUTER_PARTS - 1) + k)
                if k == 1:
                    ins = dve.reciprocal(r_inv[:], r_sum[:])
                elif k == 2:
                    ins = dve.tensor_tensor(r_probs[:], r_exp[:],
                                            r_inv[:].unsqueeze(2).to_broadcast([P, TILES, E]), ALU.mult)
                elif k == 3:
                    hold()
                    for i in range(TILES):
                        ins = dve.max(r_top[:, i, :], r_probs[:, i, :])
                elif k == 4:
                    dve.tensor_scalar(r_half[:], r_top[:, :, 0:2], 0.5, None, ALU.mult)
                    for i in range(TILES):
                        ins = dve.max_index(r_idx[:, i, :], r_top[:, i, :], r_probs[:, i, :])
                elif k == 5:
                    ins = dve.tensor_copy(r_idxf[:], r_idx[:, :, 0:2])
                elif k == 6:
                    for i in range(TILES):
                        dve.tensor_scalar(r_first[:, i, :], expert_no[:], r_idxf[:, i, 0:1],
                                          r_half[:, i, 0:1], ALU.is_equal, ALU.mult)
                        ins = dve.tensor_scalar(r_second[:, i, :], expert_no[:], r_idxf[:, i, 1:2],
                                                r_half[:, i, 1:2], ALU.is_equal, ALU.mult)
                elif k == 7:
                    dve.tensor_tensor(gates[:], r_first[:], r_second[:], ALU.add).then_inc(gates_done, 1)
                    return
                ins.then_inc(r_link, 1)

            def between(t, n, p, k):
                mid = 1 <= n <= SEQS
                if p == 1 and mid:
                    if k == 0:
                        dve.wait_ge(res1_done, t)
                    if k < NORM_PARTS:
                        norm_part(k, ln_link, (t - 1) * (2 * NORM_PARTS), res1)
                    if k == NORM_PARTS:
                        if n >= 2:
                            dve.wait_ge(x1_twice_done, t - 1)
                        norm_end(ln_link, (t - 1) * (2 * NORM_PARTS), res1, x1, x1_done)
                if p == 2 and mid:
                    if k == 0:
                        dve.wait_ge(x1_done, t)
                    if k < NORM_PARTS:
                        norm_part(k, ln_link, (t - 1) * (2 * NORM_PARTS) + NORM_PARTS, x1)
                    if k == NORM_PARTS:
                        norm_end(ln_link, (t - 1) * (2 * NORM_PARTS) + NORM_PARTS, x1, xn, xn_done)
                if p == 5 and mid and 1 <= k <= ROUTER_PARTS:
                    router_part(k - 1, t)
                if p == 7 and n >= 2:
                    if k == 0:
                        dve.wait_ge(res2_done, t - 1)
                    if k < NORM_PARTS:
                        norm_part(k, fin_link, (t - 2) * NORM_PARTS, res2)
                    if k == NORM_PARTS:
                        dve.wait_ge(out_sb_free, t - 1)
                        norm_end(fin_link, (t - 2) * NORM_PARTS, res2, out_sb, out_done)

            def step(t, n, p):
                g, f = g_of(t, p), f_of(t, p)
                attention, ffn = pair_in_range(n, p), pass_in_range(n, p)
                mid = 1 <= n <= SEQS
                if pair_in_range(n, p, -1):
                    dve.wait_ge(pt_hi_done, g)
                    dve.tensor_tensor(pt_lo[:], ps_pt[:, :, 0:3 * P], pt_hi[:].bitcast(F32), ALU.subtract
                                      ).then_inc(pt_lo_done, 1)
                if p == 1 and n < SEQS:
                    v_part(t, 1)
                if p == 5 and mid:
                    dve.wait_ge(logits_ready, t)
                    logits = ps_m[:, 0:TILES * E].rearrange("p (i e) -> p i e", i=TILES)
                    dve.tensor_reduce(r_negmax[:], logits, AX.X, ALU.max, negate=True
                                      ).then_inc(logits_link, 1)
                    dve.wait_ge(logits_link, t)
                    dve.tensor_tensor(r_diff[:], logits,
                                      r_negmax[:].unsqueeze(2).to_broadcast([P, TILES, E]), ALU.add
                                      ).then_inc(r_diff_done, 1)
                if p == 7 and n + 1 < SEQS:
                    split_xt(t + 1)
                between(t, n, p, 0)
                if attention:
                    dve.wait_ge(scores_ready, g + 1)
                    dve.tensor_reduce(neg_max[:, :, 0], ps_s[:, :, 0:2 * P], AX.X, ALU.max, negate=True)
                between(t, n, p, 1)
                if attention:
                    dve.tensor_reduce(neg_max[:, :, 1], ps_s[:, :, 2 * P:3 * P], AX.X, ALU.max, negate=True
                                      ).then_inc(max_done, 1)
                between(t, n, p, 2)
                if ffn:
                    hidden(t, p, 0)
                between(t, n, p, 3)
                if pass_in_range(n, p, -1):
                    e = expert(p - 1)
                    dve.wait_ge(y_ready, f)
                    if e == 0:
                        dve.wait_ge(gate_all_loaded, t * 16)
                        if n >= 2:
                            dve.wait_ge(yt_ready, t - 1)
                    if e > 1:
                        dve.wait_ge(y_sum_done, y_sums(t, p) - 1)
                    dve.tensor_tensor(y_sum[:] if e == 0 else y_gated[:], ps_y[:, 0:S],
                                      gate_all[:, :, e], ALU.mult).then_inc(y_done, 1)
                between(t, n, p, 4)
                if ffn:
                    hidden_hi(t, p, 0)
                between(t, n, p, 5)
                if attention:
                    dve.wait_ge(exp_done, g + 1)
                    dve.reciprocal(inv_sums[:], sums[:]).then_inc(inv_done, 1)
                between(t, n, p, 6)
                if attention:
                    dve.wait_ge(inv_done, g + 1)
                for h in range(2):
                    if attention:
                        dve.tensor_scalar(probs[:, h, 0:2 * P], probs[:, h, 0:2 * P],
                                          inv_sums[:, h, 0:1], None, ALU.mult)
                    between(t, n, p, 7 + h)
                    if attention:
                        ins = dve.tensor_scalar(probs[:, h, 2 * P:3 * P], probs[:, h, 2 * P:3 * P],
                                                inv_sums[:, h, 1:2], None, ALU.mult)
                if attention:
                    ins.then_inc(probs_done, 1)
                between(t, n, p, 9)
                if ffn:
                    hidden(t, p, 1)
                between(t, n, p, 10)
                if n == 0 and p >= PAIRS // 2:
                    dve.wait_ge(ffn_w_loaded, 32)
                    for e in (2 * p - PAIRS, 2 * p - PAIRS + 1):
                        dve.tensor_copy(w1_hi[:, e, :], w1_raw[:, e, :]).then_inc(ffn_w_hi, 1)
                        dve.tensor_copy(w2_hi[:, e, :], w2_raw[:, e, :]).then_inc(ffn_w_hi, 1)
                if p in (1, 2) and n < SEQS:
                    v_part(t, p + 1)
                if ffn:
                    hidden_hi(t, p, 1)
                between(t, n, p, 11)
                if p == 0 and mid:
                    dve.wait_ge(proj_ready, t)
                    dve.wait_ge(xb_done, t)
                    dve.tensor_tensor(flat(res1), ps_m[:, 0:S], flat(xb), ALU.add).then_inc(res1_done, 1)
                if p == LAG - 1 and mid:
                    dve.wait_ge(xnt_done, t)
                    if n >= 2:
                        dve.wait_ge(z_ready, (t - 1) * (2 * PAIRS))
                    dve.tensor_copy(xnt_hi[:], xnt[:]).then_inc(xnt_hi_done, 1)
                if p == LAG and n >= 2:
                    dve.wait_ge(yt_ready, t - 1)
                    dve.wait_ge(x1_twice_done, t - 1)
                    dve.tensor_tensor(flat(res2), ps_m[:, 0:S], flat(x1_twice), ALU.add
                                      ).then_inc(res2_done, 1)
                if p == 7 and n + 1 < SEQS:
                    v_part(t + 1, 0)

            iterations(dve, step)

        @block.tensor
        def _(pe):
            def product(dst, terms):
                for i, (lhs, rhs) in enumerate(terms):
                    ins = pe.matmul(dst, lhs, rhs, start=(i == 0), stop=(i == len(terms) - 1))
                return ins

            def split_terms(hi, lo, rhs_hi, rhs_lo):
                return [(hi, rhs_hi), (hi, rhs_lo), (lo, rhs_hi)]

            def transpose_tokens(src_of_tile):
                for i in range(TILES):
                    ins = pe.transpose(ps_m[:, i * P:(i + 1) * P], src_of_tile(i), ident[:])
                return ins

            def qk_projection(p):
                cols = slice(p * P, (p + 1) * P)
                for i in range(2):
                    ins = product(ps_qk[:, i, :], split_terms(wqkv_hi[:, i, cols], wqkv_lo[:, i, cols],
                                                              xt_hi[:], xt_lo[:]))
                ins.then_inc(qk_ready, 1)

            def v_projection(quarter):
                half, tile = quarter // 2, quarter % 2
                toks, cols = slice(tile * P, (tile + 1) * P), slice(half * 512, (half + 1) * 512)
                product(ps_m[:], split_terms(xt_hi[:, toks], xt_lo[:, toks], wqkv_hi[:, 2, cols],
                                             wqkv_lo[:, 2, cols])).then_inc(v_ready, 1)

            def scores():
                for h in range(2):
                    r = slice(h * DH, (h + 1) * DH)
                    pe.matmul(ps_s[:, h, 0:2 * P], qk[r, 0, P:2 * P], qk[r, 1, :], start=True, stop=True)
                for h in range(2):
                    r = slice(h * DH, (h + 1) * DH)
                    pe.matmul(ps_s[:, h, 2 * P:3 * P], qk[r, 0, 0:P], qk[r, 1, 0:P], start=False,
                              stop=True, skip_group_check=True)
                for h in range(2):
                    ins = pe.matmul(ps_s[:, h, P:3 * P], ident_bf[:], mask_bf[:].rearrange("p a b -> p (a b)"),
                                    start=False, stop=True, skip_group_check=True)
                ins.then_inc(scores_ready, 1)

            def transpose_probs():
                for h in range(2):
                    for dst, src in ((0, 2 * P), (P, 0), (2 * P, P)):
                        ins = pe.transpose(ps_pt[:, h, dst:dst + P], probs[:, h, src:src + P], ident[:])
                ins.then_inc(pt_ready, 1)

            def attention_output(p):
                cols = slice(p * P, (p + 1) * P)
                o = ps_m[:].rearrange("p (h s) -> p h s", h=2)
                k0, k1 = slice(0, 2 * P), slice(2 * P, 3 * P)
                v0h, v0l, v1h, v1l = v_hi[:, 0, cols], v_lo[:, 0, cols], v_hi[:, 1, cols], v_lo[:, 1, cols]
                pe.matmul(o, v0h, pt_hi[:, :, k0], start=True, stop=False)
                pe.matmul(o, v0h, pt_lo[:, :, k0], start=False, stop=False)
                for lhs, rhs in split_terms(v1h, v1l, pt_hi[:, :, k1], pt_lo[:, :, k1]):
                    pe.matmul(o[:, :, P:2 * P], lhs, rhs, start=False, stop=False)
                pe.matmul(o, v0l, pt_hi[:, :, k0], start=False, stop=True).then_inc(o_ready, 1)

            def hidden_projection(e, half):
                for i in range(2):
                    cols = slice((2 * half + i) * P, (2 * half + i + 1) * P)
                    ins = product(ps_z[:, i * S:(i + 1) * S],
                                  split_terms(w1_hi[:, e, cols], w1_lo[:, e, cols], xnt_hi[:], xnt_lo[:]))
                ins.then_inc(z_ready, 1)

            def expert_output(e, half):
                terms = []
                for i in range(2):
                    c = slice((2 * half + i) * D, (2 * half + i + 1) * D)
                    toks = slice(i * S, (i + 1) * S)
                    terms += split_terms(w2_hi[:, e, c], w2_lo[:, e, c], hh_hi[:, half, toks],
                                         hh_lo[:, half, toks])
                for i, (lhs, rhs) in enumerate(terms):
                    ins = pe.matmul(ps_y[:, 0:S], lhs, rhs, start=(half == 0 and i == 0),
                                    stop=(half == 1 and i == len(terms) - 1))
                if half == 1:
                    ins.then_inc(y_ready, 1)

            def wait_bank_before_attention(t, n, p):
                g = g_of(t, p)
                if p in (0, 1, 2, 3) and n < SEQS:
                    pe.wait_ge(v_lo_done, t * 4 + (p + 1))
                elif p == 4 and n >= 1:
                    pe.wait_ge(xnt_done, t)
                elif p == 5 and n >= 1:
                    pe.wait_ge(r_diff_done, t)
                elif p == 7 and n + 1 < SEQS:
                    pe.wait_ge(xt_lo_done, t + 2)
                elif p == 7 and n >= 2:
                    pe.wait_ge(res2_done, t - 1)
                else:
                    pe.wait_ge(ot_done, g - 1)

            def short_stage(t, n, p):
                g = g_of(t, p)
                mid = 1 <= n <= SEQS
                if p == 0 and mid:
                    pe.wait_ge(ot_done, g)
                    for i in range(TILES):
                        ins = product(ps_m[:, i * P:(i + 1) * P],
                                      [(ot[:, c, i * P:(i + 1) * P], wo_sb[:, c, :]) for c in range(PAIRS)])
                    ins.then_inc(proj_ready, 1)
                if p in (1, 2) and n < SEQS:
                    pe.wait_ge(ot_done, g)
                    v_projection(p + 1)
                if p == 3 and mid:
                    if n < SEQS:
                        pe.wait_ge(ot_done, g)
                    pe.wait_ge(xn_done, t)
                    transpose_tokens(lambda i: xn[:, i, :]).then_inc(xnt_ready, 1)
                if p == 4 and mid:
                    if n < SEQS:
                        pe.wait_ge(ot_done, g)
                    pe.wait_ge(xnt_done, t)
                    for i in range(TILES):
                        ins = pe.matmul(ps_m[:, i * E:(i + 1) * E], xnt[:, i * P:(i + 1) * P], rw_sb[:],
                                        start=True, stop=True)
                    ins.then_inc(logits_ready, 1)
                if p == LAG and n >= 2:
                    if n < SEQS:
                        pe.wait_ge(ot_done, g)
                    elif n == SEQS:
                        pe.wait_ge(r_diff_done, t)
                    pe.wait_ge(y_sum_done, (t - 1) * (E - 1))
                    transpose_tokens(lambda i: y_sum[:, i * P:(i + 1) * P]).then_inc(yt_ready, 1)
                if p == 7 and n + 1 < SEQS:
                    pe.wait_ge(ot_done, g)
                    v_projection(0)

            def late_stage(t, n, p):
                if p == 0 and n < SEQS:
                    if n >= 1:
                        pe.wait_ge(res1_done, t)
                    else:
                        pe.wait_ge(v_lo_done, 1)
                    v_projection(1)
                if p == 6 and n + 1 < SEQS:
                    if n >= 2:
                        pe.wait_ge(res2_done, t - 1)
                    else:
                        pe.wait_ge(ot_done, g_of(t, p))
                    pe.wait_ge(x_loaded, t * 16 + 32)
                    transpose_tokens(lambda i: x_raw[:, i, :]).then_inc(xt_ready, 1)

            def step(t, n, p):
                g, f, e = g_of(t, p), f_of(t, p), expert(p)
                if pair_in_range(n, p):
                    pe.wait_ge(qk_done, g + 1)
                    if not (n == 0 and p == 0):
                        pe.wait_ge(exp_done, g)
                    scores()
                if pass_in_range(n, p):
                    if p == LAG:
                        pe.wait_ge(xnt_lo_done, t)
                        if n == 1:
                            pe.wait_ge(ffn_w_lo, E)
                    if not (n == 1 and p == LAG):
                        pe.wait_ge(hh_done, f * 2)
                    hidden_projection(e, 0)
                if pass_in_range(n, p, -1):
                    pe.wait_ge(hh_lo_done, f * 2)
                    expert_output(expert(p - 1), 1)
                if pair_in_range(n, p, -1):
                    pe.wait_ge(pt_lo_done, g)
                    wait_bank_before_attention(t, n, p)
                    attention_output((p - 1) % PAIRS)
                if pass_in_range(n, p):
                    pe.wait_ge(hh_done, f * 2 + 1)
                    hidden_projection(e, 1)
                if pair_in_range(n, p, 1):
                    pe.wait_ge(qk_done, g + 1)
                    if p == 7:
                        pe.wait_ge(xt_lo_done, t + 2)
                    qk_projection((p + 1) % PAIRS)
                if pass_in_range(n, p):
                    if not (n == 1 and p == LAG):
                        pe.wait_ge(y_done, f)
                    pe.wait_ge(hh_lo_done, f * 2 + 1)
                    expert_output(e, 0)
                short_stage(t, n, p)
                if pair_in_range(n, p):
                    pe.wait_ge(probs_done, g + 1)
                    transpose_probs()
                late_stage(t, n, p)

            pe.wait_ge(consts_ready, 1)
            pe.wait_ge(x_loaded, 16)
            transpose_tokens(lambda i: x_raw[:, i, :]).then_inc(xt_ready, 1)
            pe.wait_ge(attn_w_lo, 1)
            pe.wait_ge(xt_lo_done, 1)
            qk_projection(0)
            v_projection(0)
            iterations(pe, step)


def kernel(L0_attn_x, L0_attn_Wq, L0_attn_Wk, L0_attn_Wv, L0_attn_bq, L0_attn_bk, L0_attn_bv, L0_attn_Wo,
           L0_attn_bo, L0_ffn_gamma, L0_ffn_beta, L0_ffn_router_w, L0_ffn_W1, L0_ffn_W2):
    import numpy as np
    import concourse.bacc as bacc
    from concourse.bass_utils import run_bass_kernel_spmd

    def columns(a, n):
        a = np.asarray(a)
        return a.reshape(n, P, -1).transpose(1, 0, 2).reshape(P, -1)

    def by_input(w):
        w = np.asarray(w)
        return w.transpose(1, 0, 2).reshape(P, -1)

    ins = {
        "x": L0_attn_x,
        "wq": by_input(L0_attn_Wq), "wk": by_input(L0_attn_Wk), "wv": by_input(L0_attn_Wv),
        "bq": columns(L0_attn_bq, PAIRS), "bk": columns(L0_attn_bk, PAIRS), "bv": columns(L0_attn_bv, PAIRS),
        "wo": columns(L0_attn_Wo, PAIRS),
        "bo": np.broadcast_to(np.asarray(L0_attn_bo), (P, P)),
        "gamma": np.asarray(L0_ffn_gamma).reshape(P, 1), "beta": np.asarray(L0_ffn_beta).reshape(P, 1),
        "router_wt": np.asarray(L0_ffn_router_w).T,
        "w1": by_input(L0_ffn_W1),
        "w2": columns(L0_ffn_W2, np.asarray(L0_ffn_W2).size // (P * P)),
    }
    nc = bacc.Bacc("TRN2", target_bir_lowering=False, num_devices=1)
    arrays, args = {}, []
    for name, a in ins.items():
        a = np.ascontiguousarray(a)
        arrays["in_" + name] = a
        args.append(nc.dram_tensor("in_" + name, a.shape, mybir.dt.from_np(a.dtype), kind="ExternalInput").ap())
    shape = arrays["in_x"].shape
    out = nc.dram_tensor("out_x", shape, F32, kind="ExternalOutput").ap()
    postln_block(nc, *args, out)
    r = run_bass_kernel_spmd(nc, [arrays], core_ids=[0])
    return r.results[0]["out_x"]
```

```python
from contextlib import ExitStack

import concourse.bass as bass
from concourse import mybir

F32 = mybir.dt.float32
F32R = mybir.dt.float32r
BF16 = mybir.dt.bfloat16
U32 = mybir.dt.uint32
I32 = mybir.dt.int32
ALU = mybir.AluOpType
ACT = mybir.ActivationFunctionType
AX = mybir.AxisListType

P = 128
LAG = 5
EPS = 1e-5
ROUTER_TEMP = 1.5
MASKED = -1e30
RSQRT_SEED = 0x5F3759DF

V_STEPS = {7: 0, 0: 1, 1: 2, 4: 3}
NEWTON_STEPS = 3
FIRST_PLACES = [(1, 0), (1, 1), (1, 4), (1, 4), (1, 6), (1, 7), (1, 8), (1, 9), (1, 10), (1, 11), (2, 0), (2, 1)]
SECOND_PLACES = [(2, 4), (2, 4), (2, 5), (2, 6), (2, 7), (2, 8), (2, 9), (2, 10), (2, 11), (3, 2), (3, 2), (3, 4)]
LAST_PLACES = [(7, 0), (7, 1), (7, 2), (7, 3), (7, 4), (7, 5), (7, 6), (7, 7), (7, 8), (7, 9), (7, 10), (7, 11)]
NORM_PARTS = 6 + 2 * NEWTON_STEPS
NORMS = ("first", "ffn", "last")
FIRST, SECOND, LAST = range(3)
SPLIT_STEPS = {(n, p): (2 * i, 2 * i + 1) for n in (0, 1) for i, p in enumerate(((3, 4, 5, 6), (0, 1, 2, 3))[n])}
PAIRS = 8


def postln_block(nc, x, wq, wk, wv, bq, bk, bv, wo, bo, gamma, beta, router_wt, w1, w2, out):
    SEQS, S, D = x.shape
    TILES = S // P
    HD = wq.shape[1]
    HEADS = 2 * PAIRS
    DH = HD // HEADS
    E = router_wt.shape[1]
    HID = w1.shape[1] // E
    CH = HID // P
    assert (S, D, DH, E, CH, TILES) == (256, P, 64, PAIRS, 4, 2)
    G = SEQS * PAIRS
    SCALE = DH ** -0.5

    gate_dram = nc.dram_tensor("gate_scratch", (S, E), F32, kind="Internal").ap()

    with ExitStack() as ctx:
        def sb(name, shape, dt=F32):
            return ctx.enter_context(nc.sbuf_tensor(name, shape, dt))

        def psum(name, shape):
            return ctx.enter_context(nc.psum_tensor(name, shape, F32))

        def sem(name):
            return ctx.enter_context(nc.semaphore(name))

        w_raw = sb("w_raw", [P, E * HID])
        wqkv_raw = w_raw[:, 0:3 * HD].rearrange("p (i n) -> p i n", i=3)
        w1_raw = w2_raw = w_raw[:].rearrange("p (e n) -> p e n", e=E)
        wqkv_hi = sb("wqkv_hi", [P, 3, HD], F32R)
        wqkv_lo = sb("wqkv_lo", [P, 3, HD], F32R)
        wo_sb = sb("wo_sb", [P, PAIRS, D])
        w1_hi = sb("w1_hi", [P, E, HID], F32R)
        w1_lo = sb("w1_lo", [P, E, HID], F32R)
        w2_hi = sb("w2_hi", [P, E, CH * D], F32R)
        w2_lo = sb("w2_lo", [P, E, CH * D], F32R)
        rw_sb = sb("rw_sb", [P, E])
        bq_raw = sb("bq_raw", [P, PAIRS])
        bq_sb = sb("bq_sb", [P, PAIRS])
        bk_sb = sb("bk_sb", [P, PAIRS])
        bv_sb = sb("bv_sb", [P, PAIRS])
        bo_sb = sb("bo_sb", [P, D])
        gamma_sb = sb("gamma_sb", [P, 1])
        beta_sb = sb("beta_sb", [P, 1])
        ident = sb("ident", [P, P])
        ident_bf = sb("ident_bf", [P, P], BF16)
        mask_bf = sb("mask_bf", [P, 2, P], BF16)
        expert_no = sb("expert_no", [P, E])
        x_raw = sb("x_raw", [P, TILES, D])
        xb = sb("xb", [P, TILES, D])
        xt_hi = sb("xt_hi", [P, S], F32R)
        xt_lo = sb("xt_lo", [P, S], F32R)
        qk = sb("qk", [P, 2, S])
        v_hi = sb("v_hi", [P, TILES, HD], F32R)
        v_lo = sb("v_lo", [P, TILES, HD], F32R)
        neg_max = sb("neg_max", [P, 2, 2])
        probs = sb("probs", [P, 2, 3 * P])
        sums = sb("sums", [P, 2, 2])
        inv_sums = sb("inv_sums", [P, 2, 2])
        pt_hi = sb("pt_hi", [P, 2, 3 * P], F32R)
        pt_lo = sb("pt_lo", [P, 2, 3 * P], F32R)
        ot = sb("ot", [P, PAIRS, S])
        res1 = sb("res1", [P, TILES, D])
        x1 = sb("x1", [P, TILES, D])
        x1_twice = sb("x1_twice", [P, TILES, D])
        xn = sb("xn", [P, TILES, D])
        xnt = sb("xnt", [P, S])
        xnt_hi = sb("xnt_hi", [P, S], F32R)
        xnt_lo = sb("xnt_lo", [P, S], F32R)
        ln_stats = sb("ln_stats", [P, TILES, 6])
        ln_mv = sb("ln_mv", [P, TILES, 2])
        ln_var = sb("ln_var", [P, TILES])
        ln_bits = sb("ln_bits", [P, TILES])
        ln_y = sb("ln_y", [P, TILES])
        ln_a = sb("ln_a", [P, TILES])
        ln_half = sb("ln_half", [P, TILES])
        waited = sb("waited", [P, 1])
        r_negmax = sb("r_negmax", [P, TILES])
        r_diff = sb("r_diff", [P, TILES, E])
        r_exp = sb("r_exp", [P, TILES, E])
        r_sum = sb("r_sum", [P, TILES])
        r_inv = sb("r_inv", [P, TILES])
        r_probs = sb("r_probs", [P, TILES, E])
        r_top = sb("r_top", [P, TILES, E])
        r_idx = sb("r_idx", [P, TILES, E], U32)
        r_idxf = sb("r_idxf", [P, TILES, 2])
        r_half = sb("r_half", [P, TILES, 2])
        r_first = sb("r_first", [P, TILES, E])
        r_second = sb("r_second", [P, TILES, E])
        gates = sb("gates", [P, TILES, E])
        gate_all = sb("gate_all", [P, S, E])
        hh = sb("hh", [P, 2, 2 * S])
        hh_hi = sb("hh_hi", [P, 2, 2, 2 * S], F32R)
        hh_lo = sb("hh_lo", [P, 2, 2, 2 * S], F32R)
        y_gated = sb("y_gated", [P, S])
        y_sum = sb("y_sum", [P, S])
        res2 = sb("res2", [P, TILES, D])
        out_sb = sb("out_sb", [P, TILES, D])

        ps_s = psum("ps_s", [P, 2, 512])
        ps_pt = psum("ps_pt", [P, 2, 512])
        ps_p = psum("ps_p", [P, 2, S])
        ps_z = psum("ps_z", [P, 2, 2 * S])
        ps_m = psum("ps_m", [P, 512])

        x_loaded = sem("x_loaded")
        attn_w_loaded = [sem("attn_w_loaded_first"), sem("attn_w_loaded_second")]
        ffn_w_loaded = sem("ffn_w_loaded")
        small_loaded = sem("small_loaded")
        wo_loaded = sem("wo_loaded")
        gates_stored = sem("gates_stored")
        gate_all_loaded = sem("gate_all_loaded")
        out_stored = sem("out_stored")
        out_sb_free = sem("out_sb_free")
        pool_const = sem("pool_const")
        consts_ready = sem("consts_ready")
        biases_ready = sem("biases_ready")
        attn_w_hi = sem("attn_w_hi")
        attn_w_lo = sem("attn_w_lo")
        ffn_w_hi = sem("ffn_w_hi")
        ffn_w_lo = sem("ffn_w_lo")
        scores_ready = sem("scores_ready")
        pt_ready = sem("pt_ready")
        o_ready = sem("o_ready")
        qk_ready = sem("qk_ready")
        z_ready = sem("z_ready")
        y_ready = sem("y_ready")
        v_ready = sem("v_ready")
        proj_ready = sem("proj_ready")
        xnt_ready = sem("xnt_ready")
        logits_ready = sem("logits_ready")
        yt_ready = sem("yt_ready")
        xt_ready = sem("xt_ready")
        exp_done = sem("exp_done")
        pt_hi_done = sem("pt_hi_done")
        ot_done = sem("ot_done")
        qk_done = sem("qk_done")
        tanh_done = sem("tanh_done")
        v_hi_done = sem("v_hi_done")
        xt_hi_done = sem("xt_hi_done")
        xnt_done = sem("xnt_done")
        r_exp_done = sem("r_exp_done")
        probs_1_done = sem("probs_1_done")
        max_done = sem("max_done")
        inv_done = sem("inv_done")
        probs_0_done = sem("probs_0_done")
        pt_lo_done = sem("pt_lo_done")
        hh_done = sem("hh_done")
        hh_hi_done = sem("hh_hi_done")
        y_done = sem("y_done")
        v_lo_done = sem("v_lo_done")
        xt_lo_done = sem("xt_lo_done")
        res1_done = sem("res1_done")
        x1_done = sem("x1_done")
        xn_done = sem("xn_done")
        xnt_hi_done = sem("xnt_hi_done")
        r_diff_done = sem("r_diff_done")
        gates_done = sem("gates_done")
        res2_done = sem("res2_done")
        out_done = sem("out_done")
        norm_link = [sem("norm_link_" + kind) for kind in NORMS]
        logits_link = sem("logits_link")
        r_link = sem("r_link")
        xb_done = sem("xb_done")
        hh_lo_done = sem("hh_lo_done")
        y_sum_done = sem("y_sum_done")
        xnt_lo_done = sem("xnt_lo_done")
        x1_twice_done = sem("x1_twice_done")

        block = ctx.enter_context(nc.Block())

        def iterations(eng, step):
            def one(t, n):
                for p in range(PAIRS):
                    step(t, n, p)
            one(0, 0)
            one(1, 1)
            with eng.Fori(2, SEQS - 1) as t:
                one(t, 2)
            one(SEQS - 1, SEQS - 1)
            one(SEQS, SEQS)
            one(SEQS + 1, SEQS + 1)

        def pair_in_range(n, p, off=0):
            return 0 <= PAIRS * n + p + off < G

        def pass_in_range(n, p, off=0):
            return 0 <= PAIRS * (n - 1) + p - LAG + off < G

        def g_of(t, p):
            return t * PAIRS + p

        def f_of(t, p):
            return t * PAIRS + (p - LAG - PAIRS)

        def expert(p):
            return (p - LAG) % PAIRS

        def v_quarter(n, p):
            quarter = V_STEPS.get(p)
            after = 1 if quarter == 0 else 0
            return (quarter, after) if quarter is not None and n + after < SEQS else None

        def parity(p):
            return (p - LAG) % 2

        def y_sums(t, p):
            return t * (E - 1) + (expert(p - 1) - (E - 1) * (1 if p > LAG else 2))

        @block.sync
        def _(sp):
            sp.dma_start(x_raw[:], x[0].rearrange("(i p) d -> p i d", p=P)).then_inc(x_loaded, 16)
            for half in range(2):
                cols = slice(half * 512, (half + 1) * 512)
                for i, w in enumerate((wq, wk, wv)):
                    sp.dma_start(wqkv_raw[:, i, cols], w[:, cols]).then_inc(attn_w_loaded[half], 16)
            sp.dma_start(wo_sb[:], wo.rearrange("p (c d) -> p c d", c=PAIRS)).then_inc(wo_loaded, 16)
            sp.wait_ge(attn_w_lo, 2)
            sp.dma_start(w_raw[:], w1).then_inc(ffn_w_loaded, 16)

            def step(t, n, p):
                if p == 4 and n + 1 < SEQS:
                    sp.wait_ge(xt_ready, t + 1)
                    sp.wait_ge(xb_done, t + 1)
                    sp.dma_start(x_raw[:], x[t + 1].rearrange("(i p) d -> p i d", p=P)
                                 ).then_inc(x_loaded, 16)
                if n == 0 and p == 7:
                    sp.wait_ge(ffn_w_lo, E)
                    sp.dma_start(w_raw[:], w2).then_inc(ffn_w_loaded, 16)
                if p == LAG and 1 <= n <= SEQS:
                    sp.wait_ge(gates_done, t)
                    sp.dma_start(gate_dram.rearrange("(i p) e -> p i e", p=P), gates[:]
                                 ).then_inc(gates_stored, 16)
                    sp.wait_ge(gates_stored, t * 16)
                    if n >= 2:
                        sp.wait_ge(y_done, (t - 1) * PAIRS)
                    sp.dma_start(gate_all[:].rearrange("p s e -> p (s e)"),
                                 gate_dram.rearrange("s e -> (s e)").partition_broadcast(P)
                                 ).then_inc(gate_all_loaded, 16)
                if p == 7 and n >= 2:
                    sp.wait_ge(out_done, t - 1)
                    sp.dma_start(out[t - 2].rearrange("(i p) d -> p i d", p=P), out_sb[:]
                                 ).then_inc(out_stored, 16)
                    sp.wait_ge(out_stored, (t - 1) * 16)
                    sp.sem_inc(out_sb_free, 1)

            sp.sem_inc(out_sb_free, 1)
            iterations(sp, step)
            sp.wait_ge(out_stored, 16 * SEQS)

        @block.gpsimd
        def _(pool):
            pool.memset(ident[:], 0.0).then_inc(pool_const, 1)
            pool.memset(mask_bf[:], 0.0).then_inc(pool_const, 1)
            for e in range(E):
                pool.memset(expert_no[:, e:e + 1], float(e))
            pool.wait_ge(pool_const, 2)
            pool.affine_select(out=ident[:], in_=ident[:], compare_op=ALU.not_equal, fill=1.0, base=0,
                               pattern=[[-1, P]], channel_multiplier=1).then_inc(pool_const, 1)
            pool.affine_select(out=mask_bf[:], in_=mask_bf[:], compare_op=ALU.is_ge, fill=MASKED, base=0,
                               pattern=[[0, 2], [-1, P]], channel_multiplier=1)
            pool.wait_ge(pool_const, 3)
            pool.tensor_copy(ident_bf[:], ident[:]).then_inc(consts_ready, 1)

            def ffn_weights_rest(i, e):
                raw, hi, lo = ((w1_raw, w1_hi, w1_lo), (w2_raw, w2_hi, w2_lo))[i]
                pool.wait_ge(ffn_w_hi, i * E + e + 1)
                pool.tensor_tensor(lo[:, e, :], raw[:, e, :], hi[:, e, :].bitcast(F32), ALU.subtract
                                   ).then_inc(ffn_w_lo, 1)

            def hidden_rest(t, p, half):
                pool.wait_ge(hh_hi_done, f_of(t, p) * 2 + (half + 1))
                par = parity(p)
                pool.tensor_tensor(hh_lo[:, par, half, :], hh[:, half, :],
                                   hh_hi[:, par, half, :].bitcast(F32), ALU.subtract
                                   ).then_inc(hh_lo_done, 1)

            def add_output(t, n, p):
                if pass_in_range(n, p, -1) and expert(p - 1) > 0:
                    if expert(p - 1) > 1:
                        pool.wait_ge(y_sum_done, y_sums(t, p) - 1)
                    pool.wait_ge(y_done, f_of(t, p))
                    pool.tensor_tensor(y_sum[:], y_sum[:], y_gated[:], ALU.add).then_inc(y_sum_done, 1)

            def step(t, n, p):
                for e in SPLIT_STEPS.get((n, p), ()):
                    ffn_weights_rest(n, e)
                if pass_in_range(n, p):
                    hidden_rest(t, p, 0)
                if p == LAG - 1 and 1 <= n <= SEQS:
                    pool.wait_ge(xnt_hi_done, t)
                    pool.tensor_tensor(xnt_lo[:], xnt[:], xnt_hi[:].bitcast(F32), ALU.subtract
                                       ).then_inc(xnt_lo_done, 1)
                if pair_in_range(n, p):
                    add_output(t, n, p)
                if p == 3 and n < SEQS:
                    if n >= 1:
                        pool.wait_ge(res1_done, t)
                    pool.wait_ge(x_loaded, t * 16 + 16)
                    for i in range(TILES):
                        ins = pool.tensor_tensor(xb[:, i, :], x_raw[:, i, :], bo_sb[:], ALU.add)
                    ins.then_inc(xb_done, 1)
                if p == 7 and 1 <= n <= SEQS:
                    pool.wait_ge(x1_done, t)
                    if n >= 2:
                        pool.wait_ge(res2_done, t - 1)
                    pool.tensor_tensor(x1_twice[:], x1[:], x1[:], ALU.add).then_inc(x1_twice_done, 1)
                if pass_in_range(n, p):
                    hidden_rest(t, p, 1)
                if not pair_in_range(n, p):
                    add_output(t, n, p)

            pool.wait_ge(small_loaded, 16 * 7)
            iterations(pool, step)

        @block.scalar
        def _(act):
            for dst, src in ((bq_raw, bq), (bk_sb, bk), (bv_sb, bv), (bo_sb, bo), (gamma_sb, gamma),
                             (beta_sb, beta), (rw_sb, router_wt)):
                act.dma_start(dst[:], src).then_inc(small_loaded, 16)

            def evacuate_qk(count, p):
                act.wait_ge(qk_ready, count)
                act.activation(qk[:, 0, :], ps_p[:, 0, :], ACT.Identity, bias=bq_sb[:, p:p + 1])
                act.activation(qk[:, 1, :], ps_p[:, 1, :], ACT.Identity, bias=bk_sb[:, p:p + 1]
                               ).then_inc(qk_done, 1)

            def v_part(t, quarter):
                half, tile = quarter // 2, quarter % 2
                act.wait_ge(v_ready, t * 4 + (quarter + 1))
                act.activation(v_hi[:, tile, half * 512:(half + 1) * 512],
                               ps_p[:].rearrange("p i s -> p (i s)"), ACT.Copy
                               ).then_inc(v_hi_done, 1)

            def split_xt(t):
                act.wait_ge(xt_ready, t + 1)
                act.activation(xt_hi[:], ps_p[:, 0, :], ACT.Copy).then_inc(xt_hi_done, 1)

            split_xt(0)
            act.wait_ge(biases_ready, 1)
            evacuate_qk(1, 0)
            v_part(0, 0)

            def tanh_half(t, n, p, half):
                if not (n == 1 and p == LAG):
                    act.wait_ge(hh_lo_done, f_of(t, p) * 2 + (half - 1))
                act.wait_ge(z_ready, f_of(t, p) * 2 + (half + 1))
                act.activation(hh[:, half, :], ps_z[:, half, :], ACT.Tanh, scale=0.5).then_inc(tanh_done, 1)

            def probs_hi(g, h):
                if h == 0:
                    act.wait_ge(pt_ready, g)
                act.activation(pt_hi[:, h, :], ps_pt[:, h, 0:3 * P], ACT.Copy).then_inc(pt_hi_done, 1)

            def step(t, n, p):
                g = g_of(t, p)
                before, attention, ffn = pair_in_range(n, p, -1), pair_in_range(n, p), pass_in_range(n, p)
                mid = 1 <= n <= SEQS
                if ffn:
                    tanh_half(t, n, p, 0)
                if pair_in_range(n, p, 1):
                    evacuate_qk(g + 2, (p + 1) % PAIRS)
                if before:
                    probs_hi(g, 0)
                    probs_hi(g, 1)
                if p == 4 and mid:
                    act.wait_ge(r_diff_done, t)
                    act.activation(r_exp[:], r_diff[:], ACT.Exp, scale=1.0 / ROUTER_TEMP
                                   ).then_inc(r_exp_done, 1)
                if attention:
                    act.wait_ge(max_done, g + 1)
                    for h in range(2):
                        act.activation(probs[:, h, 0:2 * P], ps_s[:, h, 0:2 * P], ACT.Exp,
                                       bias=neg_max[:, h, 0:1], accum_out=sums[:, h, 0:1])
                        ins = act.activation(probs[:, h, 2 * P:3 * P], ps_s[:, h, 2 * P:3 * P], ACT.Exp,
                                             bias=neg_max[:, h, 1:2], accum_out=sums[:, h, 1:2])
                    ins.then_inc(exp_done, 1)
                if ffn:
                    tanh_half(t, n, p, 1)
                if before:
                    act.wait_ge(o_ready, g)
                    q = (p - 1) % PAIRS
                    for h in range(2):
                        r = slice(h * DH, (h + 1) * DH)
                        ins = act.activation(ot[r, q, :], ps_m[r, h * S:(h + 1) * S], ACT.Identity,
                                             bias=bv_sb[r, q:q + 1])
                    ins.then_inc(ot_done, 1)
                if v_quarter(n, p):
                    quarter, after = v_quarter(n, p)
                    v_part(t + after if after else t, quarter)
                if p == 3 and mid:
                    act.wait_ge(xnt_ready, t)
                    act.activation(xnt[:], ps_p[:, 0, :], ACT.Identity, scale=gamma_sb[:, 0:1],
                                   bias=beta_sb[:, 0:1]).then_inc(xnt_done, 1)
                if p == 6 and n + 1 < SEQS:
                    split_xt(t + 1)
                if attention:
                    act.wait_ge(inv_done, g + 1)
                    act.activation(probs[:, 1, 0:2 * P], probs[:, 1, 0:2 * P], ACT.Copy,
                                   scale=inv_sums[:, 1, 0:1])
                    act.activation(probs[:, 1, 2 * P:3 * P], probs[:, 1, 2 * P:3 * P], ACT.Copy,
                                   scale=inv_sums[:, 1, 1:2]).then_inc(probs_1_done, 1)

            iterations(act, step)

        @block.vector
        def _(dve):
            dve.memset(waited[:], 0.0)
            def split_attn_weights(half):
                cols = slice(half * 512, (half + 1) * 512)
                dve.wait_ge(attn_w_loaded[half], 16 * 3)
                dve.tensor_scalar(wqkv_hi[:, 0, cols], wqkv_raw[:, 0, cols], SCALE, None, ALU.mult)
                dve.tensor_copy(wqkv_hi[:, 1:3, cols], wqkv_raw[:, 1:3, cols]).then_inc(attn_w_hi, 1)
                dve.wait_ge(attn_w_hi, half + 1)
                dve.scalar_tensor_tensor(out=wqkv_lo[:, 0, cols], in0=wqkv_raw[:, 0, cols], scalar=SCALE,
                                         in1=wqkv_hi[:, 0, cols].bitcast(F32), op0=ALU.mult,
                                         op1=ALU.subtract)
                dve.tensor_tensor(wqkv_lo[:, 1:3, cols], wqkv_raw[:, 1:3, cols],
                                  wqkv_hi[:, 1:3, cols].bitcast(F32), ALU.subtract).then_inc(attn_w_lo, 1)

            split_attn_weights(0)

            def split_xt(t):
                dve.wait_ge(xt_hi_done, t + 1)
                dve.tensor_tensor(xt_lo[:], ps_p[:, 0, :], xt_hi[:].bitcast(F32), ALU.subtract
                                  ).then_inc(xt_lo_done, 1)

            def v_part(t, quarter):
                half, tile = quarter // 2, quarter % 2
                dve.wait_ge(v_hi_done, t * 4 + (quarter + 1))
                cols = slice(half * 512, (half + 1) * 512)
                dve.tensor_tensor(v_lo[:, tile, cols], ps_p[:].rearrange("p i s -> p (i s)"),
                                  v_hi[:, tile, cols].bitcast(F32), ALU.subtract).then_inc(v_lo_done, 1)

            split_xt(0)
            dve.wait_ge(small_loaded, 16 * 7)
            dve.tensor_scalar(bq_sb[:], bq_raw[:], SCALE, None, ALU.mult).then_inc(biases_ready, 1)
            v_part(0, 0)

            def flat(tile):
                return tile[:].rearrange("p i d -> p (i d)")

            def hold():
                dve.memset(waited[:], 0.0)

            def norm_part(k, kind, count, src, dst, done):
                if k > 0:
                    dve.wait_ge(norm_link[kind], count * (NORM_PARTS - 1) + k)
                if k == 0:
                    for i in range(TILES):
                        ins = dve.bn_stats(ln_stats[:, i, :], src[:, i, :])
                elif k == 1:
                    hold()
                    for i in range(TILES):
                        ins = dve.bn_aggr(ln_mv[:, i, :], ln_stats[:, i, :])
                elif k == 2:
                    ins = dve.tensor_scalar(ln_var[:], ln_mv[:, :, 1], EPS, None, ALU.add)
                elif k == 3:
                    dve.tensor_scalar(ln_half[:], ln_var[:], -0.5, None, ALU.mult)
                    ins = dve.tensor_scalar(ln_bits[:].bitcast(I32), ln_var[:].bitcast(I32), 1, None,
                                            ALU.logical_shift_right)
                elif k == 4:
                    ins = dve.tensor_scalar(ln_y[:].bitcast(I32), ln_bits[:].bitcast(I32), -1, RSQRT_SEED,
                                            ALU.mult, ALU.add)
                elif k == NORM_PARTS - 1:
                    for i in range(TILES):
                        ins = dve.tensor_scalar(dst[:, i, :], src[:, i, :], ln_mv[:, i, 0:1],
                                                ln_y[:, i:i + 1], ALU.subtract, ALU.mult)
                elif k % 2 == 1:
                    for i in range(TILES):
                        ins = dve.scalar_tensor_tensor(out=ln_a[:, i:i + 1], in0=ln_y[:, i:i + 1],
                                                       scalar=ln_half[:, i:i + 1], in1=ln_y[:, i:i + 1],
                                                       op0=ALU.mult, op1=ALU.mult)
                else:
                    ins = dve.scalar_tensor_tensor(out=ln_y[:], in0=ln_a[:], scalar=1.5, in1=ln_y[:],
                                                   op0=ALU.add, op1=ALU.mult)
                ins.then_inc(norm_link[kind] if k + 1 < NORM_PARTS else done, 1)

            def hidden(t, p, half):
                dve.wait_ge(tanh_done, f_of(t, p) * 2 + (half + 1))
                dve.scalar_tensor_tensor(out=hh[:, half, :], in0=hh[:, half, :], scalar=1.0,
                                         in1=ps_z[:, half, :],
                                         op0=ALU.add, op1=ALU.mult).then_inc(hh_done, 1)

            def hidden_hi(t, p, half):
                dve.wait_ge(hh_done, f_of(t, p) * 2 + (half + 1))
                dve.tensor_copy(hh_hi[:, parity(p), half, :], hh[:, half, :]).then_inc(hh_hi_done, 1)

            ROUTER_PARTS = 8
            NORM_AT = {}
            for kind, places in ((FIRST, FIRST_PLACES), (SECOND, SECOND_PLACES), (LAST, LAST_PLACES)):
                for part, place in enumerate(places):
                    NORM_AT.setdefault(place, []).append((kind, part))

            def router_part(k, t):
                if k == 0:
                    dve.wait_ge(r_exp_done, t)
                    ins = dve.tensor_reduce(r_sum[:], r_exp[:], AX.X, ALU.add)
                else:
                    dve.wait_ge(r_link, (t - 1) * (ROUTER_PARTS - 1) + k)
                if k == 1:
                    ins = dve.reciprocal(r_inv[:], r_sum[:])
                elif k == 2:
                    ins = dve.tensor_tensor(r_probs[:], r_exp[:],
                                            r_inv[:].unsqueeze(2).to_broadcast([P, TILES, E]), ALU.mult)
                elif k == 3:
                    hold()
                    for i in range(TILES):
                        ins = dve.max(r_top[:, i, :], r_probs[:, i, :])
                elif k == 4:
                    dve.tensor_scalar(r_half[:], r_top[:, :, 0:2], 0.5, None, ALU.mult)
                    for i in range(TILES):
                        ins = dve.max_index(r_idx[:, i, :], r_top[:, i, :], r_probs[:, i, :])
                elif k == 5:
                    ins = dve.tensor_copy(r_idxf[:], r_idx[:, :, 0:2])
                elif k == 6:
                    for i in range(TILES):
                        dve.tensor_scalar(r_first[:, i, :], expert_no[:], r_idxf[:, i, 0:1],
                                          r_half[:, i, 0:1], ALU.is_equal, ALU.mult)
                        ins = dve.tensor_scalar(r_second[:, i, :], expert_no[:], r_idxf[:, i, 1:2],
                                                r_half[:, i, 1:2], ALU.is_equal, ALU.mult)
                elif k == 7:
                    dve.tensor_tensor(gates[:], r_first[:], r_second[:], ALU.add).then_inc(gates_done, 1)
                    return
                ins.then_inc(r_link, 1)

            def between(t, n, p, k):
                mid = 1 <= n <= SEQS
                for kind, part in NORM_AT.get((p, k), ()):
                    if kind == FIRST and mid:
                        if part == 0:
                            dve.wait_ge(res1_done, t)
                        if part == NORM_PARTS - 1 and n >= 2:
                            dve.wait_ge(x1_twice_done, t - 1)
                        norm_part(part, FIRST, t - 1, res1, x1, x1_done)
                    if kind == SECOND and mid:
                        if part == 0:
                            dve.wait_ge(x1_done, t)
                        norm_part(part, SECOND, t - 1, x1, xn, xn_done)
                    if kind == LAST and n >= 2:
                        if part == 0:
                            dve.wait_ge(res2_done, t - 1)
                        if part == NORM_PARTS - 1:
                            dve.wait_ge(out_sb_free, t - 1)
                        norm_part(part, LAST, t - 2, res2, out_sb, out_done)
                if p == 4 and mid and 4 <= k < ROUTER_PARTS + 4:
                    router_part(k - 4, t)

            def gated_output(t, n, p):
                if pass_in_range(n, p, -1):
                    e = expert(p - 1)
                    dve.wait_ge(y_ready, f_of(t, p))
                    if e == 0:
                        dve.wait_ge(gate_all_loaded, t * 16)
                        if n >= 2:
                            dve.wait_ge(yt_ready, t - 1)
                    if e > 1:
                        dve.wait_ge(y_sum_done, y_sums(t, p) - 1)
                    dve.tensor_tensor(y_sum[:] if e == 0 else y_gated[:], ps_p[:, 0, :],
                                      gate_all[:, :, e], ALU.mult).then_inc(y_done, 1)

            def step(t, n, p):
                g, f = g_of(t, p), f_of(t, p)
                before, attention, ffn = pair_in_range(n, p, -1), pair_in_range(n, p), pass_in_range(n, p)
                mid = 1 <= n <= SEQS
                if p == 1 and mid:
                    dve.wait_ge(proj_ready, t)
                    dve.wait_ge(xb_done, t)
                    dve.tensor_tensor(flat(res1), ps_m[:, 0:S], flat(xb), ALU.add).then_inc(res1_done, 1)
                if attention:
                    dve.wait_ge(scores_ready, g + 1)
                    dve.tensor_reduce(neg_max[:, :, 0], ps_s[:, :, 0:2 * P], AX.X, ALU.max, negate=True)
                between(t, n, p, 0)
                if attention:
                    dve.tensor_reduce(neg_max[:, :, 1], ps_s[:, :, 2 * P:3 * P], AX.X, ALU.max, negate=True
                                      ).then_inc(max_done, 1)
                between(t, n, p, 1)
                if p == 4 and mid:
                    dve.wait_ge(logits_ready, t)
                    logits = ps_m[:, 0:TILES * E].rearrange("p (i e) -> p i e", i=TILES)
                    dve.tensor_reduce(r_negmax[:], logits, AX.X, ALU.max, negate=True
                                      ).then_inc(logits_link, 1)
                    dve.wait_ge(logits_link, t)
                    dve.tensor_tensor(r_diff[:], logits,
                                      r_negmax[:].unsqueeze(2).to_broadcast([P, TILES, E]), ALU.add
                                      ).then_inc(r_diff_done, 1)
                if ffn:
                    hidden(t, p, 0)
                between(t, n, p, 2)
                if ffn:
                    hidden_hi(t, p, 0)
                if p == LAG + 1 and n >= 2:
                    dve.wait_ge(yt_ready, t - 1)
                    dve.wait_ge(x1_twice_done, t - 1)
                    dve.tensor_tensor(flat(res2), ps_m[:, 0:S], flat(x1_twice), ALU.add
                                      ).then_inc(res2_done, 1)
                if before:
                    dve.wait_ge(pt_hi_done, g * 2 - 1)
                    dve.tensor_tensor(pt_lo[:, 0, :], ps_pt[:, 0, 0:3 * P], pt_hi[:, 0, :].bitcast(F32),
                                      ALU.subtract).then_inc(pt_lo_done, 1)
                between(t, n, p, 3)
                if before:
                    dve.wait_ge(pt_hi_done, g * 2)
                    dve.tensor_tensor(pt_lo[:, 1, :], ps_pt[:, 1, 0:3 * P], pt_hi[:, 1, :].bitcast(F32),
                                      ALU.subtract).then_inc(pt_lo_done, 1)
                between(t, n, p, 4)
                if attention:
                    gated_output(t, n, p)
                if p == LAG - 1 and mid:
                    dve.wait_ge(xnt_done, t)
                    if n >= 2:
                        dve.wait_ge(z_ready, (t - 1) * (2 * PAIRS))
                    dve.tensor_copy(xnt_hi[:], xnt[:]).then_inc(xnt_hi_done, 1)
                between(t, n, p, 5)
                if attention:
                    dve.wait_ge(exp_done, g + 1)
                    dve.reciprocal(inv_sums[:], sums[:]).then_inc(inv_done, 1)
                between(t, n, p, 6)
                between(t, n, p, 7)
                if attention:
                    dve.wait_ge(inv_done, g + 1)
                    dve.tensor_scalar(probs[:, 0, 0:2 * P], probs[:, 0, 0:2 * P], inv_sums[:, 0, 0:1],
                                      None, ALU.mult)
                between(t, n, p, 8)
                if attention:
                    dve.tensor_scalar(probs[:, 0, 2 * P:3 * P], probs[:, 0, 2 * P:3 * P],
                                      inv_sums[:, 0, 1:2], None, ALU.mult).then_inc(probs_0_done, 1)
                between(t, n, p, 9)
                if ffn:
                    hidden(t, p, 1)
                if v_quarter(n, p):
                    quarter, after = v_quarter(n, p)
                    v_part(t + after if after else t, quarter)
                if p == 6 and n + 1 < SEQS:
                    split_xt(t + 1)
                between(t, n, p, 10)
                if ffn:
                    hidden_hi(t, p, 1)
                between(t, n, p, 11)
                if not attention:
                    gated_output(t, n, p)
                if n == 0 and p == 0:
                    split_attn_weights(1)
                for e in SPLIT_STEPS.get((n, p), ()):
                    raw, hi = ((w1_raw, w1_hi), (w2_raw, w2_hi))[n]
                    dve.wait_ge(ffn_w_loaded, 16 * n + 16)
                    dve.tensor_copy(hi[:, e, :], raw[:, e, :]).then_inc(ffn_w_hi, 1)

            iterations(dve, step)

        @block.tensor
        def _(pe):
            def product(dst, terms):
                for i, (lhs, rhs) in enumerate(terms):
                    ins = pe.matmul(dst, lhs, rhs, start=(i == 0), stop=(i == len(terms) - 1))
                return ins

            def split_terms(hi, lo, rhs_hi, rhs_lo):
                return [(hi, rhs_hi), (hi, rhs_lo), (lo, rhs_hi)]

            def transpose_tokens(dst, src_of_tile):
                for i in range(TILES):
                    ins = pe.transpose(dst[:, i * P:(i + 1) * P], src_of_tile(i), ident[:])
                return ins

            def qk_projection(p):
                cols = slice(p * P, (p + 1) * P)
                for i in range(2):
                    ins = product(ps_p[:, i, :], split_terms(wqkv_hi[:, i, cols], wqkv_lo[:, i, cols],
                                                              xt_hi[:], xt_lo[:]))
                ins.then_inc(qk_ready, 1)

            def v_projection(quarter):
                half, tile = quarter // 2, quarter % 2
                toks, cols = slice(tile * P, (tile + 1) * P), slice(half * 512, (half + 1) * 512)
                product(ps_p[:].rearrange("p i s -> p (i s)"),
                        split_terms(xt_hi[:, toks], xt_lo[:, toks], wqkv_hi[:, 2, cols],
                                             wqkv_lo[:, 2, cols])).then_inc(v_ready, 1)

            def scores():
                for h in range(2):
                    r = slice(h * DH, (h + 1) * DH)
                    pe.matmul(ps_s[:, h, 0:2 * P], qk[r, 0, P:2 * P], qk[r, 1, :], start=True, stop=True)
                for h in range(2):
                    r = slice(h * DH, (h + 1) * DH)
                    pe.matmul(ps_s[:, h, 2 * P:3 * P], qk[r, 0, 0:P], qk[r, 1, 0:P], start=False,
                              stop=True, skip_group_check=True)
                for h in range(2):
                    ins = pe.matmul(ps_s[:, h, P:3 * P], ident_bf[:], mask_bf[:].rearrange("p a b -> p (a b)"),
                                    start=False, stop=True, skip_group_check=True)
                ins.then_inc(scores_ready, 1)

            def transpose_probs():
                for h in range(2):
                    for dst, src in ((0, 2 * P), (P, 0), (2 * P, P)):
                        ins = pe.transpose(ps_pt[:, h, dst:dst + P], probs[:, h, src:src + P], ident[:])
                ins.then_inc(pt_ready, 1)

            def attention_output(g, p):
                cols = slice(p * P, (p + 1) * P)
                o = ps_m[:].rearrange("p (h s) -> p h s", h=2)
                k0, k1 = slice(0, 2 * P), slice(2 * P, 3 * P)
                v0h, v0l, v1h, v1l = v_hi[:, 0, cols], v_lo[:, 0, cols], v_hi[:, 1, cols], v_lo[:, 1, cols]
                pe.wait_ge(pt_hi_done, g * 2)
                pe.matmul(o, v0h, pt_hi[:, :, k0], start=True, stop=False)
                pe.matmul(o, v0l, pt_hi[:, :, k0], start=False, stop=False)
                for v1 in (v1h, v1l):
                    pe.matmul(o[:, :, P:2 * P], v1, pt_hi[:, :, k1], start=False, stop=False)
                pe.wait_ge(pt_lo_done, g * 2)
                pe.matmul(o[:, :, P:2 * P], v1h, pt_lo[:, :, k1], start=False, stop=False)
                pe.matmul(o, v0h, pt_lo[:, :, k0], start=False, stop=True).then_inc(o_ready, 1)

            def hidden_projection(e, half):
                for i in range(2):
                    cols = slice((2 * half + i) * P, (2 * half + i + 1) * P)
                    ins = product(ps_z[:, half, i * S:(i + 1) * S],
                                  split_terms(w1_hi[:, e, cols], w1_lo[:, e, cols], xnt_hi[:], xnt_lo[:]))
                ins.then_inc(z_ready, 1)

            def expert_output(f, e):
                def chunk(c):
                    half, toks, cols = c // 2, slice(c % 2 * S, (c % 2 + 1) * S), slice(c * D, (c + 1) * D)
                    return (w2_hi[:, e, cols], w2_lo[:, e, cols], hh_hi[:, e % 2, half, toks],
                            hh_lo[:, e % 2, half, toks])
                pe.wait_ge(hh_hi_done, f * 2)
                for c in range(CH):
                    hi, lo, rhs_hi, _ = chunk(c)
                    pe.matmul(ps_p[:, 0, :], hi, rhs_hi, start=(c == 0), stop=False)
                    pe.matmul(ps_p[:, 0, :], lo, rhs_hi, start=False, stop=False)
                pe.wait_ge(hh_lo_done, f * 2)
                for c in range(CH):
                    hi, _, _, rhs_lo = chunk(c)
                    ins = pe.matmul(ps_p[:, 0, :], hi, rhs_lo, start=False, stop=(c == CH - 1))
                ins.then_inc(y_ready, 1)

            def wait_bank_before_attention(t, n, p):
                g = g_of(t, p)
                if p == 1 and n >= 1:
                    pe.wait_ge(res1_done, t)
                elif p == 4 and n >= 1:
                    pe.wait_ge(r_diff_done, t)
                elif p == 6 and n >= 2:
                    pe.wait_ge(res2_done, t - 1)
                elif n >= 1 or p >= 2:
                    pe.wait_ge(ot_done, g - 1)

            def stage_before_attention_output(t, n, p):
                if p in (4, LAG + 1) and 1 <= n < SEQS:
                    pe.wait_ge(ot_done, g_of(t, p) - 1)
                if p == 4 and 1 <= n <= SEQS:
                    pe.wait_ge(xnt_done, t)
                    for i in range(TILES):
                        ins = pe.matmul(ps_m[:, i * E:(i + 1) * E], xnt[:, i * P:(i + 1) * P], rw_sb[:],
                                        start=True, stop=True)
                    ins.then_inc(logits_ready, 1)
                if p == LAG + 1 and n >= 2:
                    if n == SEQS:
                        pe.wait_ge(r_diff_done, t)
                    pe.wait_ge(y_sum_done, (t - 1) * (E - 1))
                    transpose_tokens(ps_m, lambda i: y_sum[:, i * P:(i + 1) * P]).then_inc(yt_ready, 1)

            def stage_after_attention_output(t, n, p):
                x_next, xn_last = p == 6 and n + 1 < SEQS, p == 3 and 1 <= n <= SEQS
                if x_next or xn_last or v_quarter(n, p):
                    if pass_in_range(n, p, -1):
                        pe.wait_ge(y_done, f_of(t, p))
                    elif pair_in_range(n, p, 1):
                        pe.wait_ge(qk_done, g_of(t, p) + 2)
                if v_quarter(n, p):
                    quarter = v_quarter(n, p)[0]
                    if n == 0 and quarter == 2:
                        pe.wait_ge(attn_w_lo, 2)
                    v_projection(quarter)
                if xn_last:
                    pe.wait_ge(xn_done, t)
                    transpose_tokens(ps_p[:, 0, :], lambda i: xn[:, i, :]).then_inc(xnt_ready, 1)
                if x_next:
                    pe.wait_ge(x_loaded, t * 16 + 32)
                    transpose_tokens(ps_p[:, 0, :], lambda i: x_raw[:, i, :]).then_inc(xt_ready, 1)
                if p == 0 and 1 <= n <= SEQS:
                    pe.wait_ge(ot_done, g_of(t, p))
                    if n == 1:
                        pe.wait_ge(wo_loaded, 16)
                    for i in range(TILES):
                        ins = product(ps_m[:, i * P:(i + 1) * P],
                                      [(ot[:, c, i * P:(i + 1) * P], wo_sb[:, c, :]) for c in range(PAIRS)])
                    ins.then_inc(proj_ready, 1)

            def step(t, n, p):
                g, f, e = g_of(t, p), f_of(t, p), expert(p)
                if pair_in_range(n, p):
                    pe.wait_ge(qk_done, g + 1)
                    if not (n == 0 and p == 0):
                        pe.wait_ge(exp_done, g)
                    scores()
                if pass_in_range(n, p):
                    if p == LAG:
                        pe.wait_ge(xnt_lo_done, t)
                        if n == 1:
                            pe.wait_ge(ffn_w_lo, 2 * E)
                    if not (n == 1 and p == LAG):
                        pe.wait_ge(hh_done, f * 2 - 1)
                    hidden_projection(e, 0)
                if pair_in_range(n, p, 1):
                    if n == 0 and p == 0:
                        pe.wait_ge(v_lo_done, 1)
                    elif p == 0 or v_quarter(n, p - 1):
                        pe.wait_ge(v_lo_done, t * 4 + (V_STEPS[(p - 1) % PAIRS] + 1))
                    elif p == 7:
                        pe.wait_ge(xt_lo_done, t + 2)
                    elif p == 4 and n >= 1:
                        pe.wait_ge(xnt_done, t)
                    elif pass_in_range(n, p, -2):
                        pe.wait_ge(y_done, f - 1)
                    if n == 0 and p == 3:
                        pe.wait_ge(attn_w_lo, 2)
                    qk_projection((p + 1) % PAIRS)
                stage_before_attention_output(t, n, p)
                if pair_in_range(n, p, -1):
                    pe.wait_ge(probs_0_done, g)
                    pe.wait_ge(probs_1_done, g)
                    transpose_probs()
                if pass_in_range(n, p):
                    if not (n == 1 and p == LAG):
                        pe.wait_ge(hh_done, f * 2)
                    hidden_projection(e, 1)
                if pass_in_range(n, p, -1):
                    if pair_in_range(n, p, 1):
                        pe.wait_ge(qk_done, g + 2)
                    elif pass_in_range(n, p, -2):
                        pe.wait_ge(y_done, f - 1)
                        if p == 4 and n <= SEQS:
                            pe.wait_ge(xnt_done, t)
                    expert_output(f, expert(p - 1))
                if pair_in_range(n, p, -1):
                    wait_bank_before_attention(t, n, p)
                    attention_output(g, (p - 1) % PAIRS)
                stage_after_attention_output(t, n, p)

            pe.wait_ge(consts_ready, 1)
            pe.wait_ge(x_loaded, 16)
            transpose_tokens(ps_p[:, 0, :], lambda i: x_raw[:, i, :]).then_inc(xt_ready, 1)
            pe.wait_ge(attn_w_lo, 1)
            pe.wait_ge(xt_lo_done, 1)
            qk_projection(0)
            pe.wait_ge(qk_done, 1)
            v_projection(0)
            iterations(pe, step)


def kernel(L0_attn_x, L0_attn_Wq, L0_attn_Wk, L0_attn_Wv, L0_attn_bq, L0_attn_bk, L0_attn_bv, L0_attn_Wo,
           L0_attn_bo, L0_ffn_gamma, L0_ffn_beta, L0_ffn_router_w, L0_ffn_W1, L0_ffn_W2):
    import numpy as np
    import concourse.bacc as bacc
    from concourse.bass_utils import run_bass_kernel_spmd

    def columns(a, n):
        a = np.asarray(a)
        return a.reshape(n, P, -1).transpose(1, 0, 2).reshape(P, -1)

    def by_input(w):
        w = np.asarray(w)
        return w.transpose(1, 0, 2).reshape(P, -1)

    ins = {
        "x": L0_attn_x,
        "wq": by_input(L0_attn_Wq), "wk": by_input(L0_attn_Wk), "wv": by_input(L0_attn_Wv),
        "bq": columns(L0_attn_bq, PAIRS), "bk": columns(L0_attn_bk, PAIRS), "bv": columns(L0_attn_bv, PAIRS),
        "wo": columns(L0_attn_Wo, PAIRS),
        "bo": np.broadcast_to(np.asarray(L0_attn_bo), (P, P)),
        "gamma": np.asarray(L0_ffn_gamma).reshape(P, 1), "beta": np.asarray(L0_ffn_beta).reshape(P, 1),
        "router_wt": np.asarray(L0_ffn_router_w).T,
        "w1": by_input(L0_ffn_W1),
        "w2": columns(L0_ffn_W2, np.asarray(L0_ffn_W2).size // (P * P)),
    }
    nc = bacc.Bacc("TRN2", target_bir_lowering=False, num_devices=1)
    arrays, args = {}, []
    for name, a in ins.items():
        a = np.ascontiguousarray(a)
        arrays["in_" + name] = a
        args.append(nc.dram_tensor("in_" + name, a.shape, mybir.dt.from_np(a.dtype), kind="ExternalInput").ap())
    shape = arrays["in_x"].shape
    out = nc.dram_tensor("out_x", shape, F32, kind="ExternalOutput").ap()
    postln_block(nc, *args, out)
    r = run_bass_kernel_spmd(nc, [arrays], core_ids=[0])
    return r.results[0]["out_x"]
```
